# Optimizing a Trainium2 kernel written in Bass

```python
import numpy as np
import jax
import jax.numpy as jnp

def _softmax(x, axis=-1):
    return jax.nn.softmax(x, axis=axis)

def _gelu(x):
    return jax.nn.gelu(x, approximate=True)

def _silu(x):
    return jax.nn.silu(x)

def _sigmoid(x):
    return jax.nn.sigmoid(x)

def _layernorm(x, axis=-1, eps=1e-05):
    m = jnp.mean(x, axis=axis, keepdims=True)
    v = jnp.var(x, axis=axis, keepdims=True)
    return (x - m) / jnp.sqrt(v + eps)

def _scatter_add(tgt, idx, src, axis=0):
    return tgt.at[idx].add(src)

def _segment_sum(src, seg, n):
    return jax.ops.segment_sum(src, seg, n)
kernel_name = 'mk_gnn_preln_d2_gnn_r16_a9a392'

def setup_inputs(seed: int=0):
    np.random.seed(seed)
    _w = jnp.asarray

    def _rec_inputs():
        import jax
        import jax.numpy as jnp
        _gk = jax.random.key(seed)
        x = -0.0001394 + 0.9999 * jax.random.normal(jax.random.fold_in(_gk, 1), (3125, 768), jnp.float32)
        src = jax.random.randint(jax.random.fold_in(_gk, 2), (50000,), 0, 3125, jnp.int32)
        dst = jnp.minimum((3125 * jax.random.uniform(jax.random.fold_in(_gk, 3), (50000,)) ** 2.0).astype(jnp.int32), 49999)
        _o = jnp.argsort(dst, stable=True)
        src = src[_o]
        dst = dst[_o]
        return (x, src, dst)
    x, src, dst = _rec_inputs()

    def _L0_gnn_setup():
        import jax, jax.numpy as jnp
        import numpy as np
        N_NODES = 3125

        def gcn_conv(x, edge_index, W, b, n_nodes):
            src = edge_index[0]
            dst = edge_index[1]
            loop = jnp.arange(n_nodes, dtype=src.dtype)
            src = jnp.concatenate([src, loop])
            dst = jnp.concatenate([dst, loop])
            deg = jax.ops.segment_sum(jnp.ones(src.shape, x.dtype), dst, num_segments=n_nodes)
            dinv = jnp.where(deg > 0, jax.lax.rsqrt(deg), jnp.zeros_like(deg))
            norm = dinv[src] * dinv[dst]
            h = x @ W.T
            msg = h[src] * norm[:, None]
            out = jax.ops.segment_sum(msg, dst, num_segments=n_nodes)
            return out + b
        key = jax.random.key(seed)
        k1, k2, k3, k4 = jax.random.split(key, 4)
        d = 768
        n_edges = 12500
        s = 1.0 / np.sqrt(d)
        return {'x': jax.random.normal(k1, (N_NODES, d), dtype=jnp.float32), 'edge_index': jax.random.randint(k2, (2, n_edges), 0, N_NODES, dtype=jnp.int64), 'W1': jax.random.normal(k3, (d, d), dtype=jnp.float32) * s, 'b1': jnp.zeros((d,), jnp.float32), 'W2': jax.random.normal(k4, (d, d), dtype=jnp.float32) * s, 'b2': jnp.zeros((d,), jnp.float32)}
    _L0_gnn_all = _L0_gnn_setup()
    _L0_gnn_in = {k: v for k, v in _L0_gnn_all.items() if k in ('W1', 'b1', 'W2', 'b2')}
    del _L0_gnn_all

    def _L1_gnn_setup():
        import jax, jax.numpy as jnp
        import numpy as np
        N_NODES = 625
        N_EDGES = 6250
        DIM = 768
        NEG_SLOPE = 0.2

        def gat_conv(x, src, dst, W, att_src, att_dst, bias, num_nodes):
            h = x @ W
            a_s = h @ att_src
            a_d = h @ att_dst
            e = jax.nn.leaky_relu(a_s[src] + a_d[dst], NEG_SLOPE)
            m = jax.ops.segment_max(e, dst, num_segments=num_nodes)
            e = jnp.exp(e - m[dst])
            denom = jax.ops.segment_sum(e, dst, num_segments=num_nodes)
            alpha = e / denom[dst]
            msg = alpha[:, None] * h[src]
            out = jax.ops.segment_sum(msg, dst, num_segments=num_nodes)
            return out + bias
        key = jax.random.key(seed)
        ks = jax.random.split(key, 12)
        s = 1.0 / np.sqrt(DIM)
        inp = {'x': jax.random.normal(ks[0], (N_NODES, DIM), dtype=jnp.float32), 'edge_index': jax.random.randint(ks[1], (2, N_EDGES), 0, N_NODES, dtype=jnp.int64), 'W1': jax.random.normal(ks[2], (DIM, DIM), dtype=jnp.float32) * s, 'att_src1': jax.random.normal(ks[3], (DIM,), dtype=jnp.float32) * s, 'att_dst1': jax.random.normal(ks[4], (DIM,), dtype=jnp.float32) * s, 'b1': jnp.zeros((DIM,), dtype=jnp.float32), 'W2': jax.random.normal(ks[5], (DIM, DIM), dtype=jnp.float32) * s, 'att_src2': jax.random.normal(ks[6], (DIM,), dtype=jnp.float32) * s, 'att_dst2': jax.random.normal(ks[7], (DIM,), dtype=jnp.float32) * s, 'b2': jnp.zeros((DIM,), dtype=jnp.float32)}
        return inp
    _L1_gnn_all = _L1_gnn_setup()
    _L1_gnn_in = {k: v for k, v in _L1_gnn_all.items() if k in ('W1', 'att_src1', 'att_dst1', 'b1', 'W2', 'att_src2', 'att_dst2', 'b2')}
    del _L1_gnn_all
    return {'x': x, 'src': src, 'dst': dst, 'L0_gnn_W1': _L0_gnn_in['W1'], 'L0_gnn_b1': _L0_gnn_in['b1'], 'L0_gnn_W2': _L0_gnn_in['W2'], 'L0_gnn_b2': _L0_gnn_in['b2'], 'L1_gnn_W1': _L1_gnn_in['W1'], 'L1_gnn_att_src1': _L1_gnn_in['att_src1'], 'L1_gnn_att_dst1': _L1_gnn_in['att_dst1'], 'L1_gnn_b1': _L1_gnn_in['b1'], 'L1_gnn_W2': _L1_gnn_in['W2'], 'L1_gnn_att_src2': _L1_gnn_in['att_src2'], 'L1_gnn_att_dst2': _L1_gnn_in['att_dst2'], 'L1_gnn_b2': _L1_gnn_in['b2']}

def reference(x, src, dst, L0_gnn_W1, L0_gnn_b1, L0_gnn_W2, L0_gnn_b2, L1_gnn_W1, L1_gnn_att_src1, L1_gnn_att_dst1, L1_gnn_b1, L1_gnn_W2, L1_gnn_att_src2, L1_gnn_att_dst2, L1_gnn_b2):
    import jax
    import jax.numpy as jnp

    def _L0_gnn_ref(x, edge_index, W1, b1, W2, b2):
        import jax, jax.numpy as jnp
        import numpy as np
        N_NODES = 3125

        def gcn_conv(x, edge_index, W, b, n_nodes):
            src = edge_index[0]
            dst = edge_index[1]
            loop = jnp.arange(n_nodes, dtype=src.dtype)
            src = jnp.concatenate([src, loop])
            dst = jnp.concatenate([dst, loop])
            deg = jax.ops.segment_sum(jnp.ones(src.shape, x.dtype), dst, num_segments=n_nodes)
            dinv = jnp.where(deg > 0, jax.lax.rsqrt(deg), jnp.zeros_like(deg))
            norm = dinv[src] * dinv[dst]
            h = x @ W.T
            msg = h[src] * norm[:, None]
            out = jax.ops.segment_sum(msg, dst, num_segments=n_nodes)
            return out + b
        h = gcn_conv(x, edge_index, W1, b1, N_NODES)
        h = jax.nn.relu(h)
        out = gcn_conv(h, edge_index, W2, b2, N_NODES)
        return out

    def _L1_gnn_ref(x, edge_index, W1, att_src1, att_dst1, b1, W2, att_src2, att_dst2, b2):
        import jax, jax.numpy as jnp
        import numpy as np
        N_NODES = 625
        N_EDGES = 6250
        DIM = 768
        NEG_SLOPE = 0.2

        def gat_conv(x, src, dst, W, att_src, att_dst, bias, num_nodes):
            h = x @ W
            a_s = h @ att_src
            a_d = h @ att_dst
            e = jax.nn.leaky_relu(a_s[src] + a_d[dst], NEG_SLOPE)
            m = jax.ops.segment_max(e, dst, num_segments=num_nodes)
            e = jnp.exp(e - m[dst])
            denom = jax.ops.segment_sum(e, dst, num_segments=num_nodes)
            alpha = e / denom[dst]
            msg = alpha[:, None] * h[src]
            out = jax.ops.segment_sum(msg, dst, num_segments=num_nodes)
            return out + bias
        n = x.shape[0]
        loops = jnp.arange(n, dtype=edge_index.dtype)
        src = jnp.concatenate([edge_index[0], loops])
        dst = jnp.concatenate([edge_index[1], loops])
        h = gat_conv(x, src, dst, W1, att_src1, att_dst1, b1, n)
        h = jax.nn.relu(h)
        out = gat_conv(h, src, dst, W2, att_src2, att_dst2, b2, n)
        return out
    edge_index = jnp.stack([src, dst])
    h = jnp.maximum(_layernorm(x, axis=-1), 0.0)
    x = x + _L0_gnn_ref(h, edge_index, L0_gnn_W1, L0_gnn_b1, L0_gnn_W2, L0_gnn_b2)
    h = jnp.maximum(_layernorm(x, axis=-1), 0.0)
    x = x + _L1_gnn_ref(h, edge_index, L1_gnn_W1, L1_gnn_att_src1, L1_gnn_att_dst1, L1_gnn_b1, L1_gnn_W2, L1_gnn_att_src2, L1_gnn_att_dst2, L1_gnn_b2)
    return x

_drawn_inputs = setup_inputs


def setup_inputs(seed=0):
    import zlib

    import numpy as np

    out = dict(_drawn_inputs(seed))
    spreads = {'L0_gnn_b1': (0.0, 0.1),
     'L0_gnn_b2': (0.0, 0.1),
     'L1_gnn_b1': (0.0, 0.1),
     'L1_gnn_b2': (0.0, 0.1)}
    factors = {'L1_gnn_att_src1': 3.668,
     'L1_gnn_att_dst1': 8.0,
     'L1_gnn_att_src2': 8.0,
     'L1_gnn_att_dst2': 64.0}
    for name, (base, spread) in spreads.items():
        noise = np.random.default_rng([zlib.crc32(name.encode()), seed]).standard_normal(out[name].shape)
        drawn = base * np.exp(spread * noise) if base else spread * noise
        out[name] = jnp.asarray(drawn.astype(out[name].dtype))
    for name, factor in factors.items():
        out[name] = (out[name] * factor).astype(out[name].dtype)
    return out
```

```python
from contextlib import ExitStack

import concourse.bass as bass
from concourse import mybir

P = 128
ALU = mybir.AluOpType
ACT = mybir.ActivationFunctionType
AX = mybir.AxisListType
F32 = mybir.dt.float32
I32 = mybir.dt.int32
BF16 = mybir.dt.bfloat16
ds = bass.ds

SLOPE = 0.2
EPS = 1e-5
FAR = -1.0e30
G = 4
R = 3
OPEN = 1
CH = 10
TBITS = 5


def build(nc, x, src, dst, W1, b1, W2, b2, Wg1, as1, ad1, bg1, Wg2, as2, ad2, bg2, out):
    N, D = x.shape
    E = src.shape[0]
    NT = -(-N // P)
    LAST = N - (NT - 1) * P
    HALF = NT // 2
    KC = D // P
    ROW = D + 4
    ONE, ASRC, EXT = D, D + 1, D + 2
    FULL, REST = E // P, E % P
    COLS = FULL + 1
    EB = -(-(COLS + 2 * G) // P)
    PAD = NT * P - 1
    NOWHERE = COLS + 1
    BIG = EB * P
    WORK = -(-(NT * -(-COLS // G) + 2 * R) // 512) * 512
    DB = 14
    BATCHES = (COLS + 1) // DB
    XC = 5
    assert 0 < REST and N % P and NT == 2 * HALF + 1 and BATCHES * DB == COLS + 1 and NT < 1 << TBITS
    assert NT % XC == 0 and BATCHES % 2 == 0

    with ExitStack() as ctx:
        def sb(name, shape, dt=F32):
            return ctx.enter_context(nc.sbuf_tensor(name, shape, dt))

        def sem(name):
            return ctx.enter_context(nc.semaphore(name))

        def sems(name, n):
            return [sem(f"{name}_{k}") for k in range(n)]

        table = nc.dram_tensor("table", [NT * P, ROW], F32)
        x1_dram = nc.dram_tensor("x1_dram", [NT * P, D], F32)

        acc = sb("acc", [P, NT, ROW])
        wbuf = sb("wbuf", [P, 2, KC, EXT])
        ring = sb("ring", [P, R, G, ROW])
        adrow = sb("adrow", [P, NT * P])
        S = sb("S", [P, R, G, P])
        M = sb("M", [P, R, G, P], BF16)
        V = sb("V", [P, G, P])
        T = sb("T", [P, G, P])
        diag = sb("diag", [P, R, P])
        cand = sb("cand", [P, R, 8])
        bB = sb("bB", [P, D])
        attB = sb("attB", [P, 2, D])
        work = sb("work", [1, WORK], I32)
        total = sb("total", [1, 1], I32)
        srcI = sb("srcI", [P, EB * P], I32)
        dstF = sb("dstF", [P, EB * P])
        idx = sb("idx", [P, R, G], I32)
        dloc = sb("dloc", [P, R, G])
        ident = sb("ident", [P, P])
        ones = sb("ones", [P, P])
        colid = sb("colid", [P, P])
        rowid = sb("rowid", [P, 1])
        tbase = sb("tbase", [P, NT])
        dinv, adT, mT, rden, lnscale, lnbias, rstd = (
            sb(name, [P, NT]) for name in ("dinv", "adT", "mT", "rden", "lnscale", "lnbias", "rstd"))
        bn = sb("bn", [P, NT, 2, 6])
        mv = sb("mv", [P, NT, 2])
        c2 = sb("c2", [P, 2, 2])
        wl = sb("wl", [P, 24])
        wli = sb("wli", [P, 2], I32)
        PS = ctx.enter_context(nc.psum_tensor("PS", [P, 8 * 512], F32))

        def banks(k, n=512):
            return PS[:, 512 * k:512 * k + n]

        zst = [ring[:, 0, b, 0:D] for b in range(2)]
        zT = [ring[:, 0, 2 + b, 0:D] for b in range(2)]
        xin = [ring[:, 1, b, 0:D] for b in range(2)]
        ybuf = [ring[:, 1, 2 + b, 0:D] for b in range(2)]
        wnat = [ring[:, c // G, c % G, 0:D] for c in range(KC)]
        eint = [ring[:, 2, k, 0:EB * P].bitcast(I32) for k in range(2)]
        eflt = [ring[:, 2, 2 + k, 0:EB * P] for k in range(2)]
        o = 0
        hot_lo, hot_hi = [], []
        for b in range(2):
            hot_lo.append(adrow[:, o:o + DB * P // 2].bitcast(BF16).rearrange("p (k e) -> p k e", k=DB))
            o += DB * P // 2
        for b in range(2):
            hot_hi.append(adrow[:, o:o + DB * 16].bitcast(BF16).rearrange("p (k e) -> p k e", k=DB))
            o += DB * 16
        iota512 = adrow[:, o:o + 512]
        dlo = bB[:, 0:EB * P // 2].bitcast(BF16)
        dhi = attB[:, 0, 0:EB * P // 2].bitcast(BF16)
        dint = attB[:, 1, 0:EB * P].bitcast(I32)
        colid_b = M[:, 0, 0, :]
        zero_b = M[:, 0, 1, :]
        earlier = diag[:, 0, :]
        flat = "p a b -> p (a b)"
        Vf, Tf = V[:].rearrange(flat), T[:].rearrange(flat)
        Sf = S[:].rearrange("p r a b -> p (r a b)")

        padded = sem("padded")
        edges_in = sem("edges_in")
        consts = sem("consts")
        prep = sem("prep")
        edges_f = sem("edges_f")
        blocks_turned = sem("blocks_turned")
        spans_diag = sem("spans_diag")
        spans_wide = sem("spans_wide")
        counts_ready = sem("counts_ready")
        offsets_ready = sem("offsets_ready")
        cover_ready = sem("cover_ready")
        items_ready = sem("items_ready")
        items_kept = sem("items_kept")
        work_ready = sem("work_ready")
        x_in = sems("x_in", NT // XC)
        hots = sems("hots", 2)
        hots_used = sems("hots_used", 2)
        degrees = sem("degrees")
        to_root = sem("to_root")
        rooted = sem("rooted")
        ln_ready = sem("ln_ready")
        scaled = sem("scaled")
        wnat_in = sem("wnat_in")
        wnat_turned = sem("wnat_turned")
        wt_kept = sem("wt_kept")
        w_in = sems("w_in", 2)
        att_in = sems("att_in", 2)
        ext_ready = sems("ext_ready", 2)
        bias_in = sems("bias_in", 4)
        stored = sems("stored", 2)
        gathered = [sems(f"gathered{l}", R) for l in range(4)]
        staged = [sem(f"staged{l}") for l in range(4)]
        idx_seen = sem("idx_seen")
        pool_done = [sem(f"pool_done{l}") for l in range(4)]
        local = [sem(f"local{l}") for l in range(4)]
        masked = [sems(f"masked{l}", R) for l in range(4)]
        steps = [sems(f"steps{l}", R) for l in range(4)]
        evac = [sems(f"evac{l}", R) for l in range(4)]
        agg_done = [sem(f"agg_done{l}") for l in range(4)]
        v_ready, u_ready, chain, m_wide, p_ready, alpha_ready = (
            {l: sem(f"{name}{l}") for l in (2, 3)}
            for name in ("v_ready", "u_ready", "chain", "m_wide", "p_ready", "alpha_ready"))
        ad_diag = sems("ad_diag", 2)
        ad_wide = sems("ad_wide", 2)
        ad_kept = sems("ad_kept", 2)
        z_pre = sems("z_pre", 2)
        z_ready = sems("z_ready", 2)
        turned = sems("turned", 2)
        zT_ready = sems("zT_ready", 2)
        multiplied = sems("multiplied", 2)
        post_dve = sems("post_dve", 2)
        post_act = sems("post_act", 2)
        post_step = sems("post_step", 2)
        xr_in = sems("xr_in", 2)
        x1r_in = sems("x1r_in", 2)
        fin = sems("fin", 2)
        fin_step = sems("fin_step", 2)
        out_stored = sems("out_stored", 2)

        tab = table.rearrange("(t p) c -> p t c", p=P)
        x1t = x1_dram.rearrange("(t p) c -> p t c", p=P)
        x_t = x[0:(NT - 1) * P, :].rearrange("(t p) d -> p t d", p=P)
        out_t = out[0:(NT - 1) * P, :].rearrange("(t p) d -> p t d", p=P)

        def tile(a, t, n=None):
            v = a[:, ds(t, 1), :] if n is None else a[:, ds(t, 1), 0:n]
            return v.rearrange("p a c -> p (a c)")

        def wide(v):
            return v.rearrange("(o d) -> o d", o=1).broadcast_to([P, D])

        opened_by = {
            "pe": [*hots_used, *turned, *multiplied, *ad_wide, *(s for l in steps for s in l)],
            "dve": [*post_dve, *fin, *(s for l in evac for s in l)],
            "sp": [*out_stored],
            "act": [*v_ready.values(), *p_ready.values(), *z_ready, *zT_ready, *post_act, *ad_kept],
        }
        def open_up(eng, group):
            for s in opened_by[group]:
                eng.sem_inc(s, 1)

        def at(l, b, u):
            return l * (HALF + 1 - b) + u

        def at_act(l, b, u):
            return at(max(l - 1, 0), b, u)

        def at_step(l, b, u):
            return at(l - 1, b, u)

        def at_ad(l, b, u):
            return at(l - 2, b, u)

        def rounds(eng):
            v = eng.value_load(total[0:1, 0:1], min_val=1, max_val=NT * -(-COLS // G))
            return eng.snap(((v + (R - 1)) * 21846) >> 16).with_bounds(min_val=1, max_val=-(-NT * -(-COLS // G) // R))

        def item(eng, q):
            v = eng.value_load(work[0:1, ds(q, 1)], min_val=0, max_val=((NOWHERE + 1) << TBITS) - 1)
            j = eng.snap(v >> TBITS).with_bounds(min_val=0, max_val=NOWHERE)
            t = eng.snap(v & ((1 << TBITS) - 1)).with_bounds(min_val=0, max_val=NT - 1)
            return j, t

        def pairs(eng, step):
            with eng.Fori(0, HALF) as i:
                for b in range(2):
                    step(b, i, 2 * i + b)
            step(0, HALF, NT - 1)

        block = ctx.enter_context(nc.Block())

        @block.sync
        def _(sp):
            open_up(sp, "sp")
            sp.wait_ge(padded, 2)
            whole = FULL // P
            rest = FULL - whole * P
            for v, e in ((dst, eint[0]), (src, eint[1])):
                e = e.rearrange("p (k e) -> p k e", k=EB)
                sp.dma_start(e[:, 0:whole, :], v[0:whole * P * P].rearrange("(k p e) -> p k e", p=P, e=P)).then_inc(edges_in, 16)
                sp.dma_start(e[0:rest, whole, :], v[whole * P * P:FULL * P].rearrange("(p e) -> p e", e=P)).then_inc(edges_in, 16)
                sp.dma_start(e[rest:rest + 1, whole, 0:REST], v[FULL * P:E].rearrange("(p e) -> p e", p=1)).then_inc(edges_in, 16)
            for c in range(KC):
                sp.dma_start(wnat[c], W1[c * P:(c + 1) * P, :]).then_inc(wnat_in, 16)
            sp.wait_ge(padded, 3)
            for k in range(NT // XC):
                n = XC if k < NT // XC - 1 else XC - 1
                sp.dma_start(acc[:, XC * k:XC * k + n, 0:D], x_t[:, XC * k:XC * k + n, :]).then_inc(x_in[k], 16)
            sp.dma_start(acc[0:LAST, NT - 1, 0:D], x[(NT - 1) * P:N, :]).then_inc(x_in[NT // XC - 1], 16)
            sp.wait_ge(wnat_turned, KC)
            for c in range(KC):
                sp.dma_start(wnat[c], W2[c * P:(c + 1) * P, :]).then_inc(wnat_in, 16)

            def store0(b, u, t):
                sp.wait_ge(scaled, t + 1)
                sp.dma_start(tile(tab, t), tile(acc, t)).then_inc(stored[b], 16)
            pairs(sp, store0)
            sp.wait_ge(degrees, 1)
            sp.dma_start(bB[:], wide(b1)).then_inc(bias_in[0], 16)

            def store_rows(l):
                def store(b, u, t):
                    sp.wait_ge(post_act[b], OPEN + at_act(l, b, u) + 1)
                    sp.dma_start(tile(tab, t), tile(acc, t)).then_inc(stored[b], 16)
                return store

            pairs(sp, store_rows(0))
            sp.dma_start(bB[:], wide(b2)).then_inc(bias_in[1], 16)
            sp.dma_start(wbuf[:, 0, :, 0:D], Wg1.rearrange("(c p) f -> p c f", p=P)).then_inc(w_in[0], 16)
            for k, a in enumerate((as1, ad1)):
                sp.dma_start(attB[:, k, :], wide(a)).then_inc(att_in[0], 16)

            sp.wait_ge(agg_done[1], 1)
            sp.wait_ge(pool_done[1], 1)

            def load_x(b, u, t):
                sp.wait_ge(post_dve[b], OPEN + at(1, b, u))
                sp.dma_start(xin[b], tile(x_t, t)).then_inc(xr_in[b], 16)

            def store_x1(b, u, t):
                sp.wait_ge(post_dve[b], OPEN + at(1, b, u) + 1)
                sp.dma_start(tile(x1t, t), tile(acc, t, D)).then_inc(stored[b], 16)

            load_x(0, 0, 0)
            load_x(1, 0, 1)
            with sp.Fori(0, HALF - 1) as i:
                for b in range(2):
                    store_x1(b, i, 2 * i + b)
                    load_x(b, i + 1, 2 * i + b + 2)
            store_x1(0, HALF - 1, NT - 3)
            sp.dma_start(xin[0][0:LAST, :], x[(NT - 1) * P:N, :]).then_inc(xr_in[0], 16)
            store_x1(1, HALF - 1, NT - 2)
            store_x1(0, HALF, NT - 1)
            sp.dma_start(bB[:], wide(bg1)).then_inc(bias_in[2], 16)
            sp.dma_start(wbuf[:, 1, :, 0:D], Wg2.rearrange("(c p) f -> p c f", p=P)).then_inc(w_in[1], 16)
            sp.wait_ge(stored[0], 16 * at(2, 0, HALF) + 16)
            sp.wait_ge(stored[1], 16 * at(2, 1, HALF))
            pairs(sp, store_rows(2))
            sp.wait_ge(ext_ready[0], 1)
            for k, a in enumerate((as2, ad2)):
                sp.dma_start(attB[:, k, :], wide(a)).then_inc(att_in[1], 16)
            pairs(sp, store_rows(3))
            sp.dma_start(bB[:], wide(bg2)).then_inc(bias_in[3], 16)

            sp.wait_ge(agg_done[3], 1)
            sp.wait_ge(pool_done[3], 1)

            def load_x1(b, u, t):
                sp.wait_ge(fin[b], OPEN + u)
                sp.dma_start(xin[b], tile(x1t, t)).then_inc(x1r_in[b], 16)

            def store_out(b, u, t):
                sp.wait_ge(fin[b], OPEN + u + 1)
                sp.dma_start(tile(out_t, t), ybuf[b]).then_inc(out_stored[b], 16)

            load_x1(0, 0, 0)
            load_x1(1, 0, 1)
            with sp.Fori(0, HALF - 1) as i:
                for b in range(2):
                    store_out(b, i, 2 * i + b)
                    load_x1(b, i + 1, 2 * i + b + 2)
            store_out(0, HALF - 1, NT - 3)
            load_x1(0, HALF, NT - 1)
            store_out(1, HALF - 1, NT - 2)
            sp.wait_ge(fin[0], OPEN + HALF + 1)
            sp.dma_start(out[(NT - 1) * P:N, :], ybuf[0][0:LAST, :]).then_inc(out_stored[0], 16)
            sp.wait_ge(out_stored[0], OPEN + 16 * (HALF + 1))
            sp.wait_ge(out_stored[1], OPEN + 16 * HALF)

        @block.gpsimd
        def _(pool):
            nc.gpsimd.memset(eint[0], PAD).then_inc(padded, 1)
            nc.gpsimd.memset(eint[1], 0).then_inc(padded, 1)
            nc.gpsimd.memset(acc[:, NT - 1, :], 0.0).then_inc(padded, 1)
            for a, pattern, m in ((colid[:], [[1, P]], 0), (rowid[:], [[0, 1]], 1), (tbase[:], [[P, NT]], 0),
                                  (colid_b, [[1, P]], 0), (iota512, [[1, 512]], 0)):
                nc.gpsimd.iota(a, pattern=pattern, base=0, channel_multiplier=m,
                               allow_small_or_imprecise_dtypes=True).then_inc(consts, 1)
            nc.gpsimd.memset(acc[:, 0:NT - 1, D:ROW], 0.0).then_inc(consts, 1)
            pool.wait_ge(work_ready, 2)
            n = rounds(pool)

            def gather(l, r, u, q):
                j, _ = item(pool, q)
                pool.wait_ge(steps[l][r], OPEN + G * u)
                nc.gpsimd.tensor_copy(idx[:, r, :], srcI[:, ds(j, G)]).then_inc(staged[l], 1)
                pool.wait_ge(staged[l], R * u + r + 1)
                nc.gpsimd.sem_inc(idx_seen, 1)
                for s in range(G):
                    nc.gpsimd.indirect_dma_start(
                        out=ring[:, r, s, :], out_offset=None, in_=table[:, :],
                        in_offset=bass.IndirectOffsetOnAxis(ap=idx[:, r, s:s + 1], axis=0),
                    ).then_inc(gathered[l][r], 16)

            for l in range(4):
                k = (0, 1, 3, 4)[l]
                pool.wait_ge(stored[0], 16 * at(k, 0, HALF) + 16)
                pool.wait_ge(stored[1], 16 * at(k, 1, HALF))
                if l == 0:
                    pool.wait_ge(wnat_turned, 2 * KC)
                for r in range(R):
                    gather(l, r, 0, r)
                with pool.Fori(0, n) as i:
                    for r in range(R):
                        gather(l, r, i + 1, R * i + R + r)
                for r in range(R):
                    pool.wait_ge(gathered[l][r], 16 * G * n + 16 * G)
                nc.gpsimd.sem_inc(pool_done[l], 1)

        @block.scalar
        def _(act):
            open_up(act, "act")
            def keep_wt(k):
                act.wait_ge(wnat_turned, k + 1)
                l, c = divmod(k, KC)
                nc.scalar.copy(wbuf[:, l, :, P * c:P * c + P],
                               banks(2 * (k % 2), D).rearrange("p (c f) -> p c f", f=P)).then_inc(wt_kept, 1)
            for k in range(KC):
                keep_wt(k)
            act.wait_ge(to_root, 1)
            nc.scalar.activation(dinv[:], lnbias[:], ACT.Sqrt).then_inc(rooted, 1)
            act.wait_ge(to_root, 2)
            nc.scalar.activation(rstd[:], lnscale[:], ACT.Sqrt).then_inc(rooted, 1)
            for k in range(KC, 2 * KC):
                keep_wt(k)
            act.wait_ge(ln_ready, 1)

            def scale0(b, u, t):
                nc.scalar.activation(tile(acc, t, D), tile(acc, t, D), ACT.Relu, bias=lnbias[:, ds(t, 1)],
                                     scale=lnscale[:, ds(t, 1)]).then_inc(scaled, 1)
            pairs(act, scale0)
            n = rounds(act)

            def far(l, r, u, q):
                act.wait_ge(masked[l][r], u + 1)
                act.wait_ge(gathered[l][r], 16 * G * u + 16 * G)
                for s in range(G):
                    last = nc.scalar.activation(V[:, s, :], M[:, r, s, :], ACT.Identity, scale=FAR,
                                                bias=ring[:, r, s, ASRC:ASRC + 1])
                last.then_inc(v_ready[l], 1)

            def weigh(l, r, u, q):
                act.wait_ge(chain[l], CH * q + CH)
                act.wait_ge(steps[l][r], OPEN + G * u)
                nc.scalar.activation(S[:, r, :, :].rearrange(flat), Tf, ACT.Exp).then_inc(p_ready[l], 1)
                nc.scalar.activation(cand[:, r, 4:5], cand[:, r, 3:4], ACT.Exp).then_inc(alpha_ready[l], 1)

            def agg(l):
                if l < 2:
                    return
                def keep_ad(b, u, t):
                    act.wait_ge(ad_wide[b], OPEN + at_ad(l, b, u) + 1)
                    nc.scalar.copy(adrow[:, ds(t * P, P)], banks(6 + b, P)).then_inc(ad_kept[b], 1)
                pairs(act, keep_ad)
                far(l, 0, 0, 0)
                weigh(l, 0, 0, 0)
                with act.Fori(0, n) as i:
                    for r in range(R):
                        q, r1, u1 = R * i + r + 1, (r + 1) % R, i + (r + 1) // R
                        far(l, r1, u1, q)
                        weigh(l, r1, u1, q)

            def linear(l):
                def z_stage(b, u, t):
                    if l == 3:
                        act.wait_ge(z_pre[b], u + 1)
                    act.wait_ge(turned[b], OPEN + at(l, b, u))
                    if l < 2:
                        ins = nc.scalar.copy(zst[b], tile(acc, t, D))
                    elif l == 2:
                        ins = nc.scalar.activation(zst[b], tile(acc, t, D), ACT.Relu, bias=lnbias[:, ds(t, 1)],
                                                   scale=lnscale[:, ds(t, 1)])
                    else:
                        ins = nc.scalar.activation(zst[b], ybuf[b], ACT.Relu)
                    ins.then_inc(z_ready[b], 1)

                def keep_zT(b, u, t):
                    act.wait_ge(turned[b], OPEN + at(l, b, u) + 1)
                    act.wait_ge(multiplied[b], OPEN + at(l, b, u))
                    nc.scalar.copy(zT[b], banks(4 + 2 * b, D)).then_inc(zT_ready[b], 1)

                def post(b, u, t):
                    if l == 0:
                        act.wait_ge(post_dve[b], OPEN + at(0, b, u) + 1)
                        nc.scalar.activation(tile(acc, t, D), ybuf[b], ACT.Relu,
                                             scale=dinv[:, ds(t, 1)]).then_inc(post_act[b], 1)
                    elif l >= 2:
                        act.wait_ge(post_dve[b], OPEN + at(l, b, u) + 1)
                        nc.scalar.copy(tile(acc, t, D), banks(2 * b, D)).then_inc(post_act[b], 1)

                if l == 2:
                    act.wait_ge(rooted, 3)
                    act.wait_ge(ln_ready, 2)
                    act.wait_ge(stored[0], 16 * at(2, 0, HALF) + 16)
                    act.wait_ge(stored[1], 16 * at(2, 1, HALF))
                else:
                    k = l if l < 2 else 2
                    act.wait_ge(agg_done[k], 1)
                    act.wait_ge(pool_done[k], 1)
                z_stage(0, 0, 0)
                z_stage(1, 0, 1)
                keep_zT(0, 0, 0)
                with act.Fori(0, HALF - 1) as i:
                    for b in range(2):
                        keep_zT(1 - b, i + b, 2 * i + b + 1)
                        z_stage(b, i + 1, 2 * i + b + 2)
                        post(b, i, 2 * i + b)
                keep_zT(1, HALF - 1, NT - 2)
                z_stage(0, HALF, NT - 1)
                post(0, HALF - 1, NT - 3)
                keep_zT(0, HALF, NT - 1)
                post(1, HALF - 1, NT - 2)
                post(0, HALF, NT - 1)
                if l == 1:
                    act.wait_ge(to_root, 3)
                    nc.scalar.activation(rstd[:], lnscale[:], ACT.Sqrt).then_inc(rooted, 1)

            agg(0)
            linear(0)
            agg(1)
            linear(1)
            linear(2)
            agg(2)
            linear(3)
            agg(3)

        @block.vector
        def _(dve):
            count = [0]

            def done(ins):
                count[0] += 1
                ins.then_inc(prep, 1)
                dve.wait_ge(prep, count[0])

            vec = nc.vector
            open_up(dve, "dve")
            dve.wait_ge(consts, 6)
            done(vec.tensor_scalar(ident[:], colid[:], rowid[:], None, ALU.is_equal))
            done(vec.memset(ones[:], 1.0))
            done(vec.tensor_scalar(earlier, colid[:], rowid[:], None, ALU.is_gt))
            done(vec.memset(zero_b, 0.0))
            dve.wait_ge(edges_in, 96)
            vec.tensor_copy(eflt[0], eint[0]).then_inc(edges_f, 1)
            vec.tensor_copy(eflt[1], eint[1]).then_inc(edges_f, 1)
            dve.wait_ge(edges_f, 2)
            e3 = eflt[0].rearrange("p (k e) -> p k e", k=EB)
            done(vec.tensor_reduce(wl[:, 0:EB], e3, AX.X, ALU.min))
            done(vec.tensor_reduce(wl[:, 4:4 + EB], e3, AX.X, ALU.max))
            for k in range(2 * EB):
                c = k if k < EB else 4 + k - EB
                ins = vec.tensor_scalar(Sf[:, P * k:P * k + P], ident[:], wl[:, c:c + 1], None, ALU.mult)
            ins.then_inc(spans_diag, 1)
            dve.wait_ge(blocks_turned, 2)
            done(vec.tensor_copy(dstF[:], banks(0)))
            vec.tensor_copy(srcI[:], banks(1)).then_inc(work_ready, 1)
            done(vec.tensor_copy(dint, dstF[:]))
            done(vec.tensor_scalar(eint[0], dint, P - 1, None, ALU.bitwise_and))
            done(vec.tensor_copy(dlo, eint[0]))
            done(vec.tensor_scalar(eint[0], dint, 7, None, ALU.logical_shift_right))
            done(vec.tensor_copy(dhi, eint[0]))
            done(vec.tensor_scalar(wl[:, 8:9], rowid[:], float(P), None, ALU.mult))
            done(vec.tensor_scalar(wl[:, 9:10], rowid[:], float(P), float(P - 1), ALU.mult, ALU.add))
            dve.wait_ge(spans_wide, 2)
            cov, tmp = Vf[:, 0:COLS], Tf[:, 0:COLS]
            done(vec.tensor_scalar(tmp, banks(3, COLS), wl[:, 8:9], None, ALU.is_ge))
            done(vec.scalar_tensor_tensor(out=cov, in0=banks(2, COLS), scalar=wl[:, 9:10], in1=tmp,
                                          op0=ALU.is_le, op1=ALU.mult))
            done(vec.scalar_tensor_tensor(out=tmp, in0=iota512[:, 0:COLS], scalar=1.0, in1=cov, op0=ALU.add, op1=ALU.mult))
            done(vec.tensor_reduce(wl[:, 10:11], tmp, AX.X, ALU.max))
            done(vec.scalar_tensor_tensor(out=tmp, in0=iota512[:, 0:COLS], scalar=-float(BIG), in1=cov, op0=ALU.add, op1=ALU.mult))
            done(vec.tensor_reduce(wl[:, 11:12], tmp, AX.X, ALU.min))
            done(vec.tensor_scalar(wl[:, 11:12], wl[:, 11:12], float(BIG), None, ALU.add))
            done(vec.tensor_tensor(wl[:, 12:13], wl[:, 10:11], wl[:, 11:12], ALU.subtract))
            done(vec.tensor_scalar(wl[:, 12:13], wl[:, 12:13], float(G - 1), 0.0, ALU.add, ALU.max))
            done(vec.tensor_copy(wli[:, 0:1], wl[:, 12:13]))
            done(vec.tensor_scalar(wli[:, 1:2], wli[:, 0:1], G.bit_length() - 1, None, ALU.logical_shift_right))
            vec.tensor_copy(wl[:, 13:14], wli[:, 1:2]).then_inc(counts_ready, 1)
            dve.wait_ge(offsets_ready, 1)
            done(vec.tensor_copy(wl[:, 14:16], banks(4, 2)))
            vec.tensor_copy(total[:], wl[0:1, 15:16]).then_inc(work_ready, 1)
            done(vec.tensor_tensor(wl[:, 16:17], wl[:, 14:15], wl[:, 13:14], ALU.add))
            shift = float(1 << TBITS)
            done(vec.scalar_tensor_tensor(out=wl[:, 17:18], in0=wl[:, 14:15], scalar=-float(G), in1=wl[:, 11:12], op0=ALU.mult, op1=ALU.add))
            done(vec.tensor_scalar(wl[:, 17:18], wl[:, 17:18], -float(NOWHERE), shift, ALU.add, ALU.mult))
            done(vec.tensor_tensor(wl[:, 17:18], wl[:, 17:18], rowid[:], ALU.add))
            done(vec.memset(wl[:, 18:19], G * shift))
            for c in range(WORK // 512):
                if c:
                    dve.wait_ge(items_kept, c)
                q = Sf[:, 0:512]
                done(vec.tensor_scalar(q, iota512, 512.0 * c, None, ALU.add))
                done(vec.tensor_scalar(Tf, q, wl[:, 14:15], None, ALU.is_ge))
                done(vec.scalar_tensor_tensor(out=Vf, in0=q, scalar=wl[:, 16:17], in1=Tf, op0=ALU.is_lt, op1=ALU.mult))
                vec.tensor_tensor(Sf[:, 512:1024], Vf, q, ALU.mult).then_inc(cover_ready, 1)
                dve.wait_ge(items_ready, c + 1)
                vec.tensor_scalar(work[:, 512 * c:512 * c + 512], PS[0:1, 5 * 512:6 * 512], NOWHERE * shift, None,
                                  ALU.add).then_inc(items_kept, 1)
            def hot(b, u, j):
                dve.wait_ge(hots_used[b], OPEN + u)
                vec.tensor_tensor(hot_lo[b], dlo[:, ds(j, DB)].unsqueeze(2).broadcast_to([P, DB, P]),
                                  colid_b.unsqueeze(1).broadcast_to([P, DB, P]), ALU.is_equal)
                vec.tensor_tensor(hot_hi[b][:, :, 0:NT], dhi[:, ds(j, DB)].unsqueeze(2).broadcast_to([P, DB, NT]),
                                  colid_b[:, 0:NT].unsqueeze(1).broadcast_to([P, DB, NT]), ALU.is_equal).then_inc(hots[b], 1)
            with dve.Fori(0, BATCHES // 2) as i:
                for b in range(2):
                    hot(b, i, (2 * i + b) * DB)
            dve.wait_ge(degrees, 1)
            vec.tensor_scalar(lnbias[:], banks(6, NT), 1.0, None, ALU.add).then_inc(to_root, 1)

            def stats(t):
                for h in range(2):
                    ins = vec.bn_stats(bn[:, ds(t, 1), h, :].rearrange("p a c -> p (a c)"),
                                       acc[:, ds(t, 1), h * (D // 2):(h + 1) * (D // 2)].rearrange("p a c -> p (a c)"))
                return ins

            def aggregate():
                for t in range(NT):
                    ins = vec.bn_aggr(mv[:, t, :], bn[:, t, :, :].rearrange("p a c -> p (a c)"))
                done(ins)
                vec.tensor_scalar(lnscale[:], mv[:, :, 1], EPS, None, ALU.add).then_inc(to_root, 1)

            for k in range(NT // XC):
                dve.wait_ge(x_in[k], 16 if k < NT // XC - 1 else 32)
                for t in range(XC * k, XC * k + XC):
                    ins = stats(t)
            done(ins)
            aggregate()
            dve.wait_ge(rooted, 1)
            done(vec.reciprocal(dinv[:], dinv[:]))
            dve.wait_ge(rooted, 2)
            done(vec.reciprocal(rstd[:], rstd[:]))
            done(vec.tensor_tensor(lnscale[:], rstd[:], dinv[:], ALU.mult))
            vec.scalar_tensor_tensor(out=lnbias[:], in0=mv[:, :, 0], scalar=-1.0, in1=lnscale[:],
                                     op0=ALU.mult, op1=ALU.mult).then_inc(ln_ready, 1)
            n = rounds(dve)

            def mask(l, r, u, q, first=False):
                j, t = item(dve, q)
                if l < 2:
                    dve.wait_ge(steps[l][r], OPEN + G * u)
                elif not first:
                    dve.wait_ge(v_ready[l], q - (R - OPEN) + 1)
                vec.tensor_scalar(dloc[:, r, :], dstF[:, ds(j, G)], tbase[:, ds(t, 1)], None,
                                  ALU.subtract).then_inc(local[l], 1)
                dve.wait_ge(local[l], R * u + r + 1)
                for s in range(G):
                    a = S[:, r, s, :] if l < 2 else M[:, r, s, :]
                    ins = vec.tensor_scalar(a, colid[:], dloc[:, r, s:s + 1], None, ALU.is_equal if l < 2 else ALU.not_equal)
                ins.then_inc(masked[l][r], 1)

            def score(l, r, u, q):
                _, t = item(dve, q)
                k = CH * q

                def link(ins, m):
                    ins.then_inc(chain[l], 1)
                    dve.wait_ge(chain[l], k + m)
                dve.wait_ge(v_ready[l], OPEN + q + 1)
                dve.wait_ge(p_ready[l], OPEN + q)
                link(vec.tensor_tensor(T[:], V[:], adrow[:, ds(t * P, P)].unsqueeze(1).broadcast_to([P, G, P]), ALU.add), 1)
                vec.scalar_tensor_tensor(out=Tf, in0=Tf, scalar=SLOPE, in1=Tf, op0=ALU.mult, op1=ALU.max).then_inc(chain[l], 1)
                dve.wait_ge(u_ready[l], q + 1)
                a = cand[:, r, :]
                link(vec.tensor_reduce(a[:, 0:1], banks(6), AX.X, ALU.max), 3)
                link(vec.tensor_tensor(a[:, 1:2], a[:, 0:1], adT[:, ds(t, 1)], ALU.add), 4)
                link(vec.scalar_tensor_tensor(out=a[:, 1:2], in0=a[:, 1:2], scalar=SLOPE, in1=a[:, 1:2], op0=ALU.mult, op1=ALU.max), 5)
                link(vec.tensor_tensor(a[:, 2:3], a[:, 1:2], mT[:, ds(t, 1)], ALU.max), 6)
                link(vec.tensor_scalar(diag[:, r, :], ident[:], a[:, 2:3], None, ALU.mult), 7)
                link(vec.tensor_tensor(a[:, 3:4], mT[:, ds(t, 1)], a[:, 2:3], ALU.subtract), 8)
                link(vec.tensor_scalar(mT[:, ds(t, 1)], a[:, 2:3], 1.0, None, ALU.mult), 9)
                dve.wait_ge(m_wide[l], q + 1)
                vec.tensor_tensor(T[:], T[:], banks(7, P).unsqueeze(1).broadcast_to([P, G, P]), ALU.subtract).then_inc(chain[l], 1)

            def evacuate(l, r, u, q):
                _, t = item(dve, q)
                dve.wait_ge(steps[l][r], OPEN + G * u + G)
                if r:
                    dve.wait_ge(evac[l][r - 1], OPEN + u + 1)
                else:
                    dve.wait_ge(evac[l][R - 1], OPEN + u)
                if l < 2:
                    ins = vec.tensor_tensor(tile(acc, t, D), tile(acc, t, D), banks(2 * r, D), ALU.add)
                else:
                    dve.wait_ge(alpha_ready[l], q + 1)
                    ins = vec.scalar_tensor_tensor(out=tile(acc, t, EXT), in0=tile(acc, t, EXT), scalar=cand[:, r, 4:5],
                                                   in1=banks(2 * r, EXT), op0=ALU.mult, op1=ALU.add)
                ins.then_inc(evac[l][r], 1)

            def agg(l):
                k = (0, 1, 3, 4)[l]
                if l >= 2:
                    def ad_to_diag(b, u, t):
                        dve.wait_ge(ad_wide[b], OPEN + at_ad(l, b, u))
                        vec.tensor_scalar(diag[:, b, :], ident[:], adT[:, ds(t, 1)], None, ALU.mult).then_inc(ad_diag[b], 1)
                    pairs(dve, ad_to_diag)
                    dve.wait_ge(ad_kept[0], OPEN + at_ad(l, 0, HALF) + 1)
                    dve.wait_ge(ad_kept[1], OPEN + at_ad(l, 1, HALF))
                dve.wait_ge(stored[0], 16 * at(k, 0, HALF) + 16)
                dve.wait_ge(stored[1], 16 * at(k, 1, HALF))
                mask(l, 0, 0, 0, first=True)
                mask(l, 1, 0, 1, first=True)
                if l >= 2:
                    score(l, 0, 0, 0)
                with dve.Fori(0, n) as i:
                    for r in range(R):
                        q = R * i + r
                        mask(l, (r + 2) % R, i + (r + 2) // R, q + 2)
                        if l >= 2:
                            score(l, (r + 1) % R, i + (r + 1) // R, q + 1)
                        evacuate(l, r, i, q)
                dve.wait_ge(evac[l][R - 1], OPEN + n)
                dve.sem_inc(agg_done[l], 1)

            def extend(k, l):
                dve.wait_ge(w_in[k], 16)
                dve.wait_ge(att_in[k], 32)
                for c in range(KC):
                    for m in range(2):
                        done(vec.tensor_tensor_reduce(out=adrow[:, 0:D], in0=wbuf[:, k, c, 0:D], in1=attB[:, m, :],
                                                      scale=1.0, scalar=0.0, op0=ALU.mult, op1=ALU.add,
                                                      accum_out=wbuf[:, k, c, D + m:D + m + 1]))
                dve.sem_inc(ext_ready[k], 1)

            def linear(l):
                if l == 1:
                    extend(0, 2)
                if l != 2:
                    dve.wait_ge(pool_done[l if l < 2 else 2], 1)
                bias = {0: 0, 1: 1, 3: 2}.get(l)
                if bias is not None:
                    dve.wait_ge(bias_in[bias], 16)
                if l == 3:
                    done(vec.reciprocal(rden[:], acc[:, :, ONE]))

                def pre(b, u, t):
                    if l == 3:
                        dve.wait_ge(z_ready[b], OPEN + at(3, b, u))
                        vec.scalar_tensor_tensor(out=ybuf[b], in0=tile(acc, t, D), scalar=rden[:, ds(t, 1)], in1=bB[:],
                                                 op0=ALU.mult, op1=ALU.add).then_inc(z_pre[b], 1)

                def post(b, u, t):
                    dve.wait_ge(multiplied[b], OPEN + at(l, b, u) + 1)
                    psum = banks(2 * b, EXT)
                    if l < 2:
                        if l == 0:
                            dve.wait_ge(post_act[b], OPEN + at_act(0, b, u))
                        ins = vec.scalar_tensor_tensor(out=ybuf[b], in0=psum[:, 0:D], scalar=dinv[:, ds(t, 1)], in1=bB[:],
                                                       op0=ALU.mult, op1=ALU.add)
                        if l == 0:
                            ins.then_inc(post_dve[b], 1)
                            return
                        ins.then_inc(post_step[b], 1)
                        dve.wait_ge(post_step[b], 2 * at_step(1, b, u) + 1)
                        dve.wait_ge(xr_in[b], 16 * u + 16)
                        vec.tensor_tensor(tile(acc, t, D), ybuf[b], xin[b], ALU.add).then_inc(post_step[b], 1)
                        dve.wait_ge(post_step[b], 2 * at_step(1, b, u) + 2)
                        stats(t).then_inc(post_dve[b], 1)
                        return
                    a = c2[:, b, :]
                    vec.tensor_copy(a, psum[:, D:D + 2]).then_inc(post_step[b], 1)
                    dve.wait_ge(post_step[b], 2 * at_step(l, b, u) + 1)
                    vec.tensor_scalar(acc[:, ds(t, 1), ASRC], a[:, 0:1], 1.0, None, ALU.mult)
                    vec.tensor_scalar(adT[:, ds(t, 1)], a[:, 1:2], 1.0, None, ALU.mult)
                    vec.tensor_tensor(mT[:, ds(t, 1)], a[:, 0:1], a[:, 1:2], ALU.add).then_inc(post_step[b], 1)
                    dve.wait_ge(post_step[b], 2 * at_step(l, b, u) + 2)
                    vec.scalar_tensor_tensor(out=mT[:, ds(t, 1)], in0=mT[:, ds(t, 1)], scalar=SLOPE, in1=mT[:, ds(t, 1)],
                                             op0=ALU.mult, op1=ALU.max).then_inc(post_dve[b], 1)

                if l >= 2:
                    done(vec.memset(acc[:, :, ONE], 1.0))
                pre(0, 0, 0)
                with dve.Fori(0, HALF) as i:
                    for b in range(2):
                        pre(1 - b, i + b, 2 * i + b + 1)
                        post(b, i, 2 * i + b)
                post(0, HALF, NT - 1)
                if l == 1:
                    dve.wait_ge(post_dve[0], OPEN + at(1, 0, HALF) + 1)
                    aggregate()
                    dve.wait_ge(rooted, 3)
                    done(vec.reciprocal(rstd[:], rstd[:]))
                    done(vec.tensor_copy(lnscale[:], rstd[:]))
                    vec.scalar_tensor_tensor(out=lnbias[:], in0=mv[:, :, 0], scalar=-1.0, in1=rstd[:],
                                             op0=ALU.mult, op1=ALU.mult).then_inc(ln_ready, 1)
                if l == 2:
                    dve.wait_ge(post_dve[0], OPEN + at(2, 0, HALF) + 1)
                    extend(1, 3)
                if l == 3:
                    dve.wait_ge(post_dve[0], OPEN + at(3, 0, HALF) + 1)

            agg(0)
            linear(0)
            agg(1)
            linear(1)
            linear(2)
            agg(2)
            linear(3)
            agg(3)
            dve.wait_ge(pool_done[3], 1)
            dve.wait_ge(bias_in[3], 16)
            done(vec.reciprocal(rden[:], acc[:, :, ONE]))

            def final(b, u, t):
                dve.wait_ge(out_stored[b], OPEN + 16 * u)
                vec.scalar_tensor_tensor(out=ybuf[b], in0=tile(acc, t, D), scalar=rden[:, ds(t, 1)], in1=bB[:],
                                         op0=ALU.mult, op1=ALU.add).then_inc(fin_step[b], 1)
                dve.wait_ge(fin_step[b], u + 1)
                dve.wait_ge(x1r_in[b], 16 * u + 16)
                vec.tensor_tensor(ybuf[b], ybuf[b], xin[b], ALU.add).then_inc(fin[b], 1)
            pairs(dve, final)

        @block.tensor
        def _(pe):
            mm = nc.tensor.matmul
            open_up(pe, "pe")
            pe.wait_ge(prep, 4)
            pe.wait_ge(edges_f, 2)
            for k in range(2):
                for c in range(EB):
                    ins = nc.tensor.transpose(banks(k)[:, P * c:P * c + P], eflt[k][:, P * c:P * c + P], ident[:])
                ins.then_inc(blocks_turned, 1)
            pe.wait_ge(spans_diag, 1)
            for k in range(2):
                for c in range(EB):
                    o = P * (EB * k + c)
                    ins = mm(banks(2 + k)[:, P * c:P * c + P], ones[:], Sf[:, o:o + P], start=True, stop=True)
                ins.then_inc(spans_wide, 1)
            pe.wait_ge(counts_ready, 1)
            mm(banks(4)[:, 0:1], earlier, wl[:, 13:14], start=True, stop=True)
            mm(banks(4)[:, 1:2], ones[:], wl[:, 13:14], start=True, stop=True).then_inc(offsets_ready, 1)
            for c in range(WORK // 512):
                pe.wait_ge(cover_ready, c + 1)
                o = PS[0:1, 5 * 512:6 * 512]
                mm(o, wl[:, 17:18], Vf, start=True, stop=False)
                mm(o, wl[:, 18:19], Sf[:, 512:1024], start=False, stop=True).then_inc(items_ready, 1)

            def turn_w(k):
                pe.wait_ge(wnat_in, 16 * KC * (1 + k // KC))
                if k >= 2:
                    pe.wait_ge(wt_kept, k - 1)
                for c in range(KC):
                    ins = nc.tensor.transpose(banks(2 * (k % 2), D)[:, P * c:P * c + P], wnat[k % KC][:, P * c:P * c + P], ident[:])
                ins.then_inc(wnat_turned, 1)
            pe.wait_ge(items_kept, WORK // 512)
            for k in range(KC):
                turn_w(k)

            mm(banks(6, NT), zero_b, colid_b[:, 0:NT], start=True, stop=False)
            with pe.Fori(0, BATCHES // 2) as i:
                for b in range(2):
                    pe.wait_ge(hots[b], i + 1)
                    for k in range(DB):
                        ins = mm(banks(6, NT), hot_lo[b][:, k, :], hot_hi[b][:, k, 0:NT], start=False, stop=False)
                    ins.then_inc(hots_used[b], 1)
            mm(banks(6, NT), zero_b, colid_b[:, 0:NT], start=False, stop=True).then_inc(degrees, 1)
            for k in range(KC, 2 * KC):
                turn_w(k)
            pe.wait_ge(wt_kept, 2 * KC)
            n = rounds(pe)

            def product(l, r, u, s):
                width = D if l < 2 else EXT
                mm(banks(2 * r), S[:, r, s, :], ring[:, r, s, 0:512], start=(s == 0), stop=(s == G - 1))
                mm(banks(2 * r + 1, width - 512), S[:, r, s, :], ring[:, r, s, 512:width],
                   start=(s == 0), stop=(s == G - 1)).then_inc(steps[l][r], 1)

            def turn_v(l, q):
                pe.wait_ge(v_ready[l], OPEN + q + 1)
                for s in range(G):
                    ins = nc.tensor.transpose(banks(6)[:, P * s:P * s + P], V[:, s, :], ident[:])
                ins.then_inc(u_ready[l], 1)

            def widen_m(l, r, q):
                pe.wait_ge(chain[l], CH * q + 7)
                mm(banks(7, P), ones[:], diag[:, r, :], start=True, stop=True).then_inc(m_wide[l], 1)

            def agg(l):
                if l >= 2:
                    def widen_ad(b, u, t):
                        pe.wait_ge(ad_diag[b], at_ad(l, b, u) + 1)
                        pe.wait_ge(ad_kept[b], OPEN + at_ad(l, b, u))
                        mm(banks(6 + b, P), ones[:], diag[:, b, :], start=True, stop=True).then_inc(ad_wide[b], 1)
                    pairs(pe, widen_ad)
                    turn_v(l, 0)
                    widen_m(l, 0, 0)
                with pe.Fori(0, n) as i:
                    for r in range(R):
                        q = R * i + r
                        if l < 2:
                            pe.wait_ge(masked[l][r], i + 1)
                        else:
                            pe.wait_ge(p_ready[l], OPEN + q + 1)
                        pe.wait_ge(evac[l][r], OPEN + i)
                        pe.wait_ge(gathered[l][r], 16 * G * i + 16 * G)
                        product(l, r, i, 0)
                        if l >= 2:
                            turn_v(l, q + 1)
                        product(l, r, i, 1)
                        product(l, r, i, 2)
                        if l >= 2:
                            widen_m(l, (r + 1) % R, q + 1)
                        product(l, r, i, 3)

            def linear(l):
                width = D if l < 2 else EXT

                def turn_z(b, u):
                    pe.wait_ge(z_ready[b], OPEN + at(l, b, u) + 1)
                    pe.wait_ge(zT_ready[b], OPEN + at(l, b, u))
                    for c in range(KC):
                        ins = nc.tensor.transpose(banks(4 + 2 * b, D)[:, P * c:P * c + P], zst[b][:, P * c:P * c + P], ident[:])
                    ins.then_inc(turned[b], 1)

                def multiply(b, u):
                    pe.wait_ge(zT_ready[b], OPEN + at(l, b, u) + 1)
                    pe.wait_ge(post_dve[b], OPEN + at(l, b, u))
                    if l >= 2:
                        pe.wait_ge(post_act[b], OPEN + at_act(l, b, u))
                    for c in range(KC):
                        z = zT[b][:, P * c:P * c + P]
                        mm(banks(2 * b), z, wbuf[:, l % 2, c, 0:512], start=(c == 0), stop=(c == KC - 1))
                        ins = mm(banks(2 * b + 1, width - 512), z, wbuf[:, l % 2, c, 512:width],
                                 start=(c == 0), stop=(c == KC - 1))
                    ins.then_inc(multiplied[b], 1)

                if l >= 2:
                    pe.wait_ge(ext_ready[l - 2], 1)
                turn_z(0, 0)
                with pe.Fori(0, HALF) as i:
                    for b in range(2):
                        turn_z(1 - b, i + b)
                        multiply(b, i)
                multiply(0, HALF)

            agg(0)
            linear(0)
            agg(1)
            linear(1)
            linear(2)
            agg(2)
            linear(3)
            agg(3)


def kernel(x, src, dst, L0_gnn_W1, L0_gnn_b1, L0_gnn_W2, L0_gnn_b2, L1_gnn_W1, L1_gnn_att_src1, L1_gnn_att_dst1,
           L1_gnn_b1, L1_gnn_W2, L1_gnn_att_src2, L1_gnn_att_dst2, L1_gnn_b2):
    import numpy as np
    import concourse.bacc as bacc
    from concourse.bass_utils import run_bass_kernel_spmd

    given = {
        "x": x, "src": src, "dst": dst,
        "W1": L0_gnn_W1, "b1": L0_gnn_b1, "W2": L0_gnn_W2, "b2": L0_gnn_b2,
        "Wg1": L1_gnn_W1, "as1": L1_gnn_att_src1, "ad1": L1_gnn_att_dst1, "bg1": L1_gnn_b1,
        "Wg2": L1_gnn_W2, "as2": L1_gnn_att_src2, "ad2": L1_gnn_att_dst2, "bg2": L1_gnn_b2,
    }
    nc = bacc.Bacc("TRN2", target_bir_lowering=False, num_devices=1)
    arrays = {f"in_{k}": np.ascontiguousarray(v) for k, v in given.items()}
    args = [nc.dram_tensor(k, a.shape, mybir.dt.from_np(a.dtype), kind="ExternalInput").ap() for k, a in arrays.items()]
    out = nc.dram_tensor("out", arrays["in_x"].shape, F32, kind="ExternalOutput").ap()
    build(nc, *args, out)
    r = run_bass_kernel_spmd(nc, [arrays], core_ids=[0])
    return r.results[0]["out"]
```

```python
from contextlib import ExitStack

import concourse.bass as bass
from concourse import mybir

P = 128
ALU = mybir.AluOpType
ACT = mybir.ActivationFunctionType
AX = mybir.AxisListType
F32 = mybir.dt.float32
I32 = mybir.dt.int32
BF16 = mybir.dt.bfloat16
ds = bass.ds

SLOPE = 0.2
EPS = 1e-5
FAR = -1.0e30
G = 4
RING = (3, 3, 4, 4)
OPEN = 1
CH = 9
TBITS = 5


def build(nc, x, src, dst, W1, b1, W2, b2, Wg1, as1, ad1, bg1, Wg2, as2, ad2, bg2, out):
    N, D = x.shape
    E = src.shape[0]
    NT = -(-N // P)
    LAST = N - (NT - 1) * P
    HALF = NT // 2
    KC = D // P
    ROW = D + 4
    ONE, ASRC, EXT = D, D + 1, D + 2
    FULL, REST = E // P, E % P
    COLS = FULL + 1
    EB = -(-(COLS + 2 * G) // P)
    PAD = NT * P - 1
    NOWHERE = COLS + 1
    BIG = EB * P
    WORK = -(-(NT * -(-COLS // G) + 2 * max(RING) + 1) // 512) * 512
    DB = 14
    BATCHES = (COLS + 1) // DB
    XC = 5
    assert 0 < REST and N % P and NT == 2 * HALF + 1 and BATCHES * DB == COLS + 1 and NT < 1 << TBITS
    assert NT % XC == 0 and BATCHES % 2 == 0

    with ExitStack() as ctx:
        def sb(name, shape, dt=F32):
            return ctx.enter_context(nc.sbuf_tensor(name, shape, dt))

        def sem(name):
            return ctx.enter_context(nc.semaphore(name))

        def sems(name, n):
            return [sem(f"{name}_{k}") for k in range(n)]

        table = nc.dram_tensor("table", [NT * P, ROW], F32)
        x1_dram = nc.dram_tensor("x1_dram", [NT * P, D], F32)

        acc = sb("acc", [P, NT, ROW])
        wbuf = sb("wbuf", [P, 2, KC, EXT])
        ring = sb("ring", [P, 3, G, ROW])
        adrow = sb("adrow", [P, NT * P])
        S = sb("S", [P, 3, G, P])
        V = sb("V", [P, G, P])
        T = sb("T", [P, G, P])
        diag = sb("diag", [P, 2, P])
        cand = sb("cand", [P, 4, 4])
        colid_b = sb("colid_b", [P, P], BF16)
        zero_b = sb("zero_b", [P, P], BF16)
        bB = sb("bB", [P, D])
        attB = sb("attB", [P, 2, D])
        work = sb("work", [1, WORK], I32)
        total = sb("total", [1, 1], I32)
        srcI = sb("srcI", [P, EB * P], I32)
        dstF = sb("dstF", [P, EB * P])
        idx = sb("idx", [P, 4, G], I32)
        dloc = sb("dloc", [P, 4, G])
        ident = sb("ident", [P, P])
        ones = sb("ones", [P, P])
        colid = sb("colid", [P, P])
        rowid = sb("rowid", [P, 1])
        tbase = sb("tbase", [P, NT])
        dinv, adT, top, mT, rden, lnscale, lnbias, rstd = (
            sb(name, [P, NT]) for name in ("dinv", "adT", "top", "mT", "rden", "lnscale", "lnbias", "rstd"))
        bn = sb("bn", [P, NT, 2, 6])
        mv = sb("mv", [P, NT, 2])
        c2 = sb("c2", [P, 2, 2])
        wl = sb("wl", [P, 24])
        wli = sb("wli", [P, 2], I32)
        PS = ctx.enter_context(nc.psum_tensor("PS", [P, 8 * 512], F32))

        def banks(k, n=512):
            return PS[:, 512 * k:512 * k + n]

        zst = [ring[:, 0, b, 0:D] for b in range(2)]
        zT = [ring[:, 0, 2 + b, 0:D] for b in range(2)]
        xin = [ring[:, 1, b, 0:D] for b in range(2)]
        ybuf = [ring[:, 1, 2 + b, 0:D] for b in range(2)]
        wnat = [ring[:, c // G, c % G, 0:D] for c in range(KC)]
        eint = [ring[:, 2, k, 0:EB * P].bitcast(I32) for k in range(2)]
        eflt = [ring[:, 2, 2 + k, 0:EB * P] for k in range(2)]
        o = 0
        hot_lo, hot_hi = [], []
        for b in range(2):
            hot_lo.append(adrow[:, o:o + DB * P // 2].bitcast(BF16).rearrange("p (k e) -> p k e", k=DB))
            o += DB * P // 2
        for b in range(2):
            hot_hi.append(adrow[:, o:o + DB * 16].bitcast(BF16).rearrange("p (k e) -> p k e", k=DB))
            o += DB * 16
        iota512 = adrow[:, o:o + 512]
        dlo = bB[:, 0:EB * P // 2].bitcast(BF16)
        dhi = attB[:, 0, 0:EB * P // 2].bitcast(BF16)
        dint = attB[:, 1, 0:EB * P].bitcast(I32)
        earlier = diag[:, 0, :]
        flat = "p a b -> p (a b)"
        Vf, Tf = V[:].rearrange(flat), T[:].rearrange(flat)
        spare = wbuf[:, 0, :, :].rearrange(flat)
        def carve(o, n):
            return spare[:, o:o + n * G].rearrange("p (a b) -> p a b", a=G)
        rows = [ring[:, r, :, :] for r in range(3)] + [carve(0, ROW)]
        sel = [S[:, r, :, :] for r in range(3)] + [carve(G * ROW, P)]
        logits = [T[:], carve(G * (ROW + P), P)]
        o = G * (ROW + 2 * P)
        apart = spare[:, o:o + G * P // 2].bitcast(BF16).rearrange("p (a b) -> p a b", a=G)
        assert o + G * P // 2 <= KC * EXT
        Sf = S[:].rearrange("p r a b -> p (r a b)")

        padded = sem("padded")
        edges_in = sem("edges_in")
        consts = sem("consts")
        prep = sem("prep")
        edges_f = sem("edges_f")
        blocks_turned = sem("blocks_turned")
        spans_diag = sem("spans_diag")
        spans_wide = sem("spans_wide")
        counts_ready = sem("counts_ready")
        offsets_ready = sem("offsets_ready")
        cover_ready = sem("cover_ready")
        items_ready = sem("items_ready")
        items_kept = sem("items_kept")
        work_ready = sem("work_ready")
        x_in = sems("x_in", NT // XC)
        hots = sems("hots", 2)
        hots_used = sems("hots_used", 2)
        degrees = sem("degrees")
        to_root = sem("to_root")
        rooted = sem("rooted")
        ln_ready = sem("ln_ready")
        scaled = sem("scaled")
        wnat_in = sem("wnat_in")
        wnat_turned = sem("wnat_turned")
        wt_kept = sem("wt_kept")
        w_in = sems("w_in", 2)
        att_in = sems("att_in", 2)
        ext_ready = sems("ext_ready", 2)
        bias_in = sems("bias_in", 4)
        stored = sems("stored", 2)
        gathered = [sems(f"gathered{l}", RING[l]) for l in range(4)]
        staged = [sem(f"staged{l}") for l in range(4)]
        idx_seen = sem("idx_seen")
        pool_done = [sem(f"pool_done{l}") for l in range(4)]
        local = [sem(f"local{l}") for l in range(4)]
        masked = [sem(f"masked{l}") for l in range(2)]
        steps = [sem(f"steps{l}") for l in range(4)]
        evac = [sem(f"evac{l}") for l in range(4)]
        agg_done = [sem(f"agg_done{l}") for l in range(4)]
        squared, v_ready, u_ready, chain, m_wide, p_ready, alpha_ready = (
            {l: sem(f"{name}{l}") for l in (2, 3)}
            for name in ("squared", "v_ready", "u_ready", "chain", "m_wide", "p_ready", "alpha_ready"))
        ad_diag = sems("ad_diag", 2)
        ad_wide = sems("ad_wide", 2)
        ad_kept = sems("ad_kept", 2)
        z_pre = sems("z_pre", 2)
        z_ready = sems("z_ready", 2)
        turned = sems("turned", 2)
        zT_ready = sems("zT_ready", 2)
        multiplied = sems("multiplied", 2)
        post_dve = sems("post_dve", 2)
        post_act = sems("post_act", 2)
        post_step = sems("post_step", 2)
        xr_in = sems("xr_in", 2)
        x1r_in = sems("x1r_in", 2)
        fin = sems("fin", 2)
        fin_step = sems("fin_step", 2)
        out_stored = sems("out_stored", 2)

        tab = table.rearrange("(t p) c -> p t c", p=P)
        x1t = x1_dram.rearrange("(t p) c -> p t c", p=P)
        x_t = x[0:(NT - 1) * P, :].rearrange("(t p) d -> p t d", p=P)
        out_t = out[0:(NT - 1) * P, :].rearrange("(t p) d -> p t d", p=P)

        def tile(a, t, n=None):
            v = a[:, ds(t, 1), :] if n is None else a[:, ds(t, 1), 0:n]
            return v.rearrange("p a c -> p (a c)")

        def wide(v):
            return v.rearrange("(o d) -> o d", o=1).broadcast_to([P, D])

        STEPS0 = [G * r for r in RING]
        BANKS = (3, 3, 2, 2)
        opened_by = {
            "pe": [(s, OPEN) for s in (*hots_used, *turned, *multiplied, *ad_wide)] + list(zip(steps, STEPS0)),
            "dve": [(s, OPEN) for s in (*post_dve, *fin)] + list(zip(evac, BANKS)),
            "sp": [(s, OPEN) for s in out_stored],
            "act": [(s, OPEN) for s in (*z_ready, *zT_ready, *post_act, *ad_kept)] + [(s, 2) for s in p_ready.values()],
        }
        def open_up(eng, group):
            for s, n in opened_by[group]:
                eng.sem_inc(s, n)

        def at(l, b, u):
            return l * (HALF + 1 - b) + u

        def at_act(l, b, u):
            return at(max(l - 1, 0), b, u)

        def at_step(l, b, u):
            return at(l - 1, b, u)

        def at_ad(l, b, u):
            return at(l - 2, b, u)

        def rounds(eng, l):
            v = eng.value_load(total[0:1, 0:1], min_val=1, max_val=NT * -(-COLS // G))
            most = -(-NT * -(-COLS // G) // RING[l])
            if RING[l] == 4:
                return eng.snap((v + 3) >> 2).with_bounds(min_val=1, max_val=most)
            return eng.snap(((v + 2) * 21846) >> 16).with_bounds(min_val=1, max_val=most)

        def item(eng, q):
            v = eng.value_load(work[0:1, ds(q, 1)], min_val=0, max_val=((NOWHERE + 1) << TBITS) - 1)
            j = eng.snap(v >> TBITS).with_bounds(min_val=0, max_val=NOWHERE)
            t = eng.snap(v & ((1 << TBITS) - 1)).with_bounds(min_val=0, max_val=NT - 1)
            return j, t

        def pairs(eng, step):
            with eng.Fori(0, HALF) as i:
                for b in range(2):
                    step(b, i, 2 * i + b)
            step(0, HALF, NT - 1)

        block = ctx.enter_context(nc.Block())

        @block.sync
        def _(sp):
            open_up(sp, "sp")
            sp.wait_ge(padded, 2)
            whole = FULL // P
            rest = FULL - whole * P
            for v, e in ((dst, eint[0]), (src, eint[1])):
                e = e.rearrange("p (k e) -> p k e", k=EB)
                sp.dma_start(e[:, 0:whole, :], v[0:whole * P * P].rearrange("(k p e) -> p k e", p=P, e=P)).then_inc(edges_in, 16)
                sp.dma_start(e[0:rest, whole, :], v[whole * P * P:FULL * P].rearrange("(p e) -> p e", e=P)).then_inc(edges_in, 16)
                sp.dma_start(e[rest:rest + 1, whole, 0:REST], v[FULL * P:E].rearrange("(p e) -> p e", p=1)).then_inc(edges_in, 16)
            for c in range(KC):
                sp.dma_start(wnat[c], W1[c * P:(c + 1) * P, :]).then_inc(wnat_in, 16)
            sp.wait_ge(padded, 3)
            for k in range(NT // XC):
                n = XC if k < NT // XC - 1 else XC - 1
                sp.dma_start(acc[:, XC * k:XC * k + n, 0:D], x_t[:, XC * k:XC * k + n, :]).then_inc(x_in[k], 16)
            sp.dma_start(acc[0:LAST, NT - 1, 0:D], x[(NT - 1) * P:N, :]).then_inc(x_in[NT // XC - 1], 16)
            sp.wait_ge(wnat_turned, KC)
            for c in range(KC):
                sp.dma_start(wnat[c], W2[c * P:(c + 1) * P, :]).then_inc(wnat_in, 16)

            def store0(b, u, t):
                sp.wait_ge(scaled, t + 1)
                sp.dma_start(tile(tab, t), tile(acc, t)).then_inc(stored[b], 16)
            pairs(sp, store0)
            sp.wait_ge(degrees, 1)
            sp.dma_start(bB[:], wide(b1)).then_inc(bias_in[0], 16)

            def store_rows(l):
                def store(b, u, t):
                    sp.wait_ge(post_act[b], OPEN + at_act(l, b, u) + 1)
                    sp.dma_start(tile(tab, t), tile(acc, t)).then_inc(stored[b], 16)
                return store

            pairs(sp, store_rows(0))
            sp.dma_start(bB[:], wide(b2)).then_inc(bias_in[1], 16)
            sp.dma_start(wbuf[:, 0, :, 0:D], Wg1.rearrange("(c p) f -> p c f", p=P)).then_inc(w_in[0], 16)
            for k, a in enumerate((as1, ad1)):
                sp.dma_start(attB[:, k, :], wide(a)).then_inc(att_in[0], 16)

            sp.wait_ge(agg_done[1], 1)
            sp.wait_ge(pool_done[1], 1)

            def load_x(b, u, t):
                sp.wait_ge(post_dve[b], OPEN + at(1, b, u))
                sp.dma_start(xin[b], tile(x_t, t)).then_inc(xr_in[b], 16)

            def store_x1(b, u, t):
                sp.wait_ge(post_dve[b], OPEN + at(1, b, u) + 1)
                sp.dma_start(tile(x1t, t), tile(acc, t, D)).then_inc(stored[b], 16)

            load_x(0, 0, 0)
            load_x(1, 0, 1)
            with sp.Fori(0, HALF - 1) as i:
                for b in range(2):
                    store_x1(b, i, 2 * i + b)
                    load_x(b, i + 1, 2 * i + b + 2)
            store_x1(0, HALF - 1, NT - 3)
            sp.dma_start(xin[0][0:LAST, :], x[(NT - 1) * P:N, :]).then_inc(xr_in[0], 16)
            store_x1(1, HALF - 1, NT - 2)
            store_x1(0, HALF, NT - 1)
            sp.dma_start(bB[:], wide(bg1)).then_inc(bias_in[2], 16)
            sp.dma_start(wbuf[:, 1, :, 0:D], Wg2.rearrange("(c p) f -> p c f", p=P)).then_inc(w_in[1], 16)
            sp.wait_ge(stored[0], 16 * at(2, 0, HALF) + 16)
            sp.wait_ge(stored[1], 16 * at(2, 1, HALF))
            pairs(sp, store_rows(2))
            sp.wait_ge(ext_ready[0], 1)
            for k, a in enumerate((as2, ad2)):
                sp.dma_start(attB[:, k, :], wide(a)).then_inc(att_in[1], 16)
            pairs(sp, store_rows(3))
            sp.dma_start(bB[:], wide(bg2)).then_inc(bias_in[3], 16)

            sp.wait_ge(agg_done[3], 1)
            sp.wait_ge(pool_done[3], 1)

            def load_x1(b, u, t):
                sp.wait_ge(fin[b], OPEN + u)
                sp.dma_start(xin[b], tile(x1t, t)).then_inc(x1r_in[b], 16)

            def store_out(b, u, t):
                sp.wait_ge(fin[b], OPEN + u + 1)
                sp.dma_start(tile(out_t, t), ybuf[b]).then_inc(out_stored[b], 16)

            load_x1(0, 0, 0)
            load_x1(1, 0, 1)
            with sp.Fori(0, HALF - 1) as i:
                for b in range(2):
                    store_out(b, i, 2 * i + b)
                    load_x1(b, i + 1, 2 * i + b + 2)
            store_out(0, HALF - 1, NT - 3)
            load_x1(0, HALF, NT - 1)
            store_out(1, HALF - 1, NT - 2)
            sp.wait_ge(fin[0], OPEN + HALF + 1)
            sp.dma_start(out[(NT - 1) * P:N, :], ybuf[0][0:LAST, :]).then_inc(out_stored[0], 16)
            sp.wait_ge(out_stored[0], OPEN + 16 * (HALF + 1))
            sp.wait_ge(out_stored[1], OPEN + 16 * HALF)

        @block.gpsimd
        def _(pool):
            nc.gpsimd.memset(eint[0], PAD).then_inc(padded, 1)
            nc.gpsimd.memset(eint[1], 0).then_inc(padded, 1)
            nc.gpsimd.memset(acc[:, NT - 1, :], 0.0).then_inc(padded, 1)
            for a, pattern, m in ((colid[:], [[1, P]], 0), (rowid[:], [[0, 1]], 1), (tbase[:], [[P, NT]], 0),
                                  (colid_b[:], [[1, P]], 0), (iota512, [[1, 512]], 0)):
                nc.gpsimd.iota(a, pattern=pattern, base=0, channel_multiplier=m,
                               allow_small_or_imprecise_dtypes=True).then_inc(consts, 1)
            nc.gpsimd.memset(acc[:, 0:NT - 1, D:ROW], 0.0).then_inc(consts, 1)
            pool.wait_ge(work_ready, 2)

            def gather(l, r, q, j):
                pool.wait_ge(steps[l], G * q + (G if l < 2 else 1))
                nc.gpsimd.tensor_copy(idx[:, r, :], srcI[:, ds(j, G)]).then_inc(staged[l], 1)
                pool.wait_ge(staged[l], q + 1)
                for s in range(G):
                    if l >= 2 and s:
                        pool.wait_ge(steps[l], G * q + s + 1)
                    if l >= 2 or s == 0:
                        nc.gpsimd.sem_inc(idx_seen, 1)
                    nc.gpsimd.indirect_dma_start(
                        out=rows[r][:, s, :], out_offset=None, in_=table[:, :],
                        in_offset=bass.IndirectOffsetOnAxis(ap=idx[:, r, s:s + 1], axis=0),
                    ).then_inc(gathered[l][r], 16)

            for l in range(4):
                k = (0, 1, 3, 4)[l]
                n = rounds(pool, l)
                pool.wait_ge(stored[0], 16 * at(k, 0, HALF) + 16)
                pool.wait_ge(stored[1], 16 * at(k, 1, HALF))
                if l == 0:
                    pool.wait_ge(wnat_turned, 2 * KC)
                for r in range(RING[l]):
                    gather(l, r, r, item(pool, r)[0])
                with pool.Fori(0, n) as i:
                    for r in range(RING[l]):
                        q = RING[l] * (i + 1) + r
                        gather(l, r, q, item(pool, q)[0])
                for r in range(RING[l]):
                    pool.wait_ge(gathered[l][r], 16 * G * n + 16 * G)
                nc.gpsimd.sem_inc(pool_done[l], 1)

        @block.scalar
        def _(act):
            open_up(act, "act")
            def keep_wt(k):
                act.wait_ge(wnat_turned, k + 1)
                l, c = divmod(k, KC)
                nc.scalar.copy(wbuf[:, l, :, P * c:P * c + P],
                               banks(2 * (k % 2), D).rearrange("p (c f) -> p c f", f=P)).then_inc(wt_kept, 1)
            for k in range(KC):
                keep_wt(k)
            act.wait_ge(to_root, 1)
            nc.scalar.activation(dinv[:], lnbias[:], ACT.Sqrt).then_inc(rooted, 1)
            act.wait_ge(to_root, 2)
            nc.scalar.activation(rstd[:], lnscale[:], ACT.Sqrt).then_inc(rooted, 1)
            for k in range(KC, 2 * KC):
                keep_wt(k)
            act.wait_ge(ln_ready, 1)

            def scale0(b, u, t):
                nc.scalar.activation(tile(acc, t, D), tile(acc, t, D), ACT.Relu, bias=lnbias[:, ds(t, 1)],
                                     scale=lnscale[:, ds(t, 1)]).then_inc(scaled, 1)
            pairs(act, scale0)

            def far(l, r, u, q, first=False):
                act.wait_ge(local[l], q + 1)
                if not first:
                    act.wait_ge(v_ready[l], q)
                for s in range(G):
                    last = nc.scalar.activation(apart[:, s, :], colid[:], ACT.Square, scale=-1.0,
                                                bias=dloc[:, r, s:s + 1])
                last.then_inc(squared[l], 1)
                act.wait_ge(squared[l], q + 1)
                act.wait_ge(gathered[l][r], 16 * G * u + 16 * G)
                if not first:
                    act.wait_ge(chain[l], CH * q - CH + 1)
                    act.wait_ge(u_ready[l], q)
                for s in range(G):
                    last = nc.scalar.activation(V[:, s, :], apart[:, s, :], ACT.Identity, scale=FAR,
                                                bias=rows[r][:, s, ASRC:ASRC + 1])
                last.then_inc(v_ready[l], 1)

            def weigh(l, r, q):
                act.wait_ge(chain[l], CH * q + CH)
                act.wait_ge(steps[l], G * q + G)
                nc.scalar.activation(sel[r].rearrange(flat), logits[r % 2].rearrange(flat), ACT.Exp).then_inc(p_ready[l], 1)
                nc.scalar.activation(cand[:, r, 3:4], cand[:, r, 2:3], ACT.Exp).then_inc(alpha_ready[l], 1)

            def agg(l):
                if l < 2:
                    return
                def keep_ad(b, u, t):
                    act.wait_ge(ad_wide[b], OPEN + at_ad(l, b, u) + 1)
                    nc.scalar.copy(adrow[:, ds(t * P, P)], banks(6 + b, P)).then_inc(ad_kept[b], 1)
                pairs(act, keep_ad)
                n = rounds(act, l)
                far(l, 0, 0, 0, first=True)
                far(l, 1, 0, 1)
                weigh(l, 0, 0)
                far(l, 2, 0, 2)
                weigh(l, 1, 1)
                with act.Fori(0, n) as i:
                    for r in range(4):
                        far(l, (r + 3) % 4, i + (r + 3) // 4, 4 * i + r + 3)
                        weigh(l, (r + 2) % 4, 4 * i + r + 2)

            def linear(l):
                def z_stage(b, u, t):
                    if l == 3:
                        act.wait_ge(z_pre[b], u + 1)
                    act.wait_ge(turned[b], OPEN + at(l, b, u))
                    if l < 2:
                        ins = nc.scalar.copy(zst[b], tile(acc, t, D))
                    elif l == 2:
                        ins = nc.scalar.activation(zst[b], tile(acc, t, D), ACT.Relu, bias=lnbias[:, ds(t, 1)],
                                                   scale=lnscale[:, ds(t, 1)])
                    else:
                        ins = nc.scalar.activation(zst[b], ybuf[b], ACT.Relu)
                    ins.then_inc(z_ready[b], 1)

                def keep_zT(b, u, t):
                    act.wait_ge(turned[b], OPEN + at(l, b, u) + 1)
                    act.wait_ge(multiplied[b], OPEN + at(l, b, u))
                    nc.scalar.copy(zT[b], banks(4 + 2 * b, D)).then_inc(zT_ready[b], 1)

                def post(b, u, t):
                    if l == 0:
                        act.wait_ge(post_dve[b], OPEN + at(0, b, u) + 1)
                        nc.scalar.activation(tile(acc, t, D), ybuf[b], ACT.Relu,
                                             scale=dinv[:, ds(t, 1)]).then_inc(post_act[b], 1)
                    elif l >= 2:
                        act.wait_ge(post_dve[b], OPEN + at(l, b, u) + 1)
                        nc.scalar.copy(tile(acc, t, D), banks(2 * b, D)).then_inc(post_act[b], 1)

                if l == 2:
                    act.wait_ge(rooted, 3)
                    act.wait_ge(ln_ready, 2)
                    act.wait_ge(stored[0], 16 * at(2, 0, HALF) + 16)
                    act.wait_ge(stored[1], 16 * at(2, 1, HALF))
                else:
                    k = l if l < 2 else 2
                    act.wait_ge(agg_done[k], 1)
                    act.wait_ge(pool_done[k], 1)
                z_stage(0, 0, 0)
                z_stage(1, 0, 1)
                keep_zT(0, 0, 0)
                with act.Fori(0, HALF - 1) as i:
                    for b in range(2):
                        keep_zT(1 - b, i + b, 2 * i + b + 1)
                        z_stage(b, i + 1, 2 * i + b + 2)
                        post(b, i, 2 * i + b)
                keep_zT(1, HALF - 1, NT - 2)
                z_stage(0, HALF, NT - 1)
                post(0, HALF - 1, NT - 3)
                keep_zT(0, HALF, NT - 1)
                post(1, HALF - 1, NT - 2)
                post(0, HALF, NT - 1)
                if l == 1:
                    act.wait_ge(to_root, 3)
                    nc.scalar.activation(rstd[:], lnscale[:], ACT.Sqrt).then_inc(rooted, 1)

            agg(0)
            linear(0)
            agg(1)
            linear(1)
            linear(2)
            agg(2)
            linear(3)
            agg(3)

        @block.vector
        def _(dve):
            count = [0]

            def done(ins):
                count[0] += 1
                ins.then_inc(prep, 1)
                dve.wait_ge(prep, count[0])

            vec = nc.vector
            open_up(dve, "dve")
            dve.wait_ge(consts, 6)
            done(vec.tensor_scalar(ident[:], colid[:], rowid[:], None, ALU.is_equal))
            done(vec.memset(ones[:], 1.0))
            done(vec.tensor_scalar(earlier, colid[:], rowid[:], None, ALU.is_gt))
            done(vec.memset(zero_b[:], 0.0))
            dve.wait_ge(edges_in, 96)
            vec.tensor_copy(eflt[0], eint[0]).then_inc(edges_f, 1)
            vec.tensor_copy(eflt[1], eint[1]).then_inc(edges_f, 1)
            dve.wait_ge(edges_f, 2)
            e3 = eflt[0].rearrange("p (k e) -> p k e", k=EB)
            done(vec.tensor_reduce(wl[:, 0:EB], e3, AX.X, ALU.min))
            done(vec.tensor_reduce(wl[:, 4:4 + EB], e3, AX.X, ALU.max))
            for k in range(2 * EB):
                c = k if k < EB else 4 + k - EB
                ins = vec.tensor_scalar(Sf[:, P * k:P * k + P], ident[:], wl[:, c:c + 1], None, ALU.mult)
            ins.then_inc(spans_diag, 1)
            dve.wait_ge(blocks_turned, 2)
            done(vec.tensor_copy(dstF[:], banks(0)))
            vec.tensor_copy(srcI[:], banks(1)).then_inc(work_ready, 1)
            done(vec.tensor_copy(dint, dstF[:]))
            done(vec.tensor_scalar(eint[0], dint, P - 1, None, ALU.bitwise_and))
            done(vec.tensor_copy(dlo, eint[0]))
            done(vec.tensor_scalar(eint[0], dint, 7, None, ALU.logical_shift_right))
            done(vec.tensor_copy(dhi, eint[0]))
            done(vec.tensor_scalar(wl[:, 8:9], rowid[:], float(P), None, ALU.mult))
            done(vec.tensor_scalar(wl[:, 9:10], rowid[:], float(P), float(P - 1), ALU.mult, ALU.add))
            dve.wait_ge(spans_wide, 2)
            cov, tmp = Vf[:, 0:COLS], Tf[:, 0:COLS]
            done(vec.tensor_scalar(tmp, banks(3, COLS), wl[:, 8:9], None, ALU.is_ge))
            done(vec.scalar_tensor_tensor(out=cov, in0=banks(2, COLS), scalar=wl[:, 9:10], in1=tmp,
                                          op0=ALU.is_le, op1=ALU.mult))
            done(vec.scalar_tensor_tensor(out=tmp, in0=iota512[:, 0:COLS], scalar=1.0, in1=cov, op0=ALU.add, op1=ALU.mult))
            done(vec.tensor_reduce(wl[:, 10:11], tmp, AX.X, ALU.max))
            done(vec.scalar_tensor_tensor(out=tmp, in0=iota512[:, 0:COLS], scalar=-float(BIG), in1=cov, op0=ALU.add, op1=ALU.mult))
            done(vec.tensor_reduce(wl[:, 11:12], tmp, AX.X, ALU.min))
            done(vec.tensor_scalar(wl[:, 11:12], wl[:, 11:12], float(BIG), None, ALU.add))
            done(vec.tensor_tensor(wl[:, 12:13], wl[:, 10:11], wl[:, 11:12], ALU.subtract))
            done(vec.tensor_scalar(wl[:, 12:13], wl[:, 12:13], float(G - 1), 0.0, ALU.add, ALU.max))
            done(vec.tensor_copy(wli[:, 0:1], wl[:, 12:13]))
            done(vec.tensor_scalar(wli[:, 1:2], wli[:, 0:1], G.bit_length() - 1, None, ALU.logical_shift_right))
            vec.tensor_copy(wl[:, 13:14], wli[:, 1:2]).then_inc(counts_ready, 1)
            dve.wait_ge(offsets_ready, 1)
            done(vec.tensor_copy(wl[:, 14:16], banks(4, 2)))
            vec.tensor_copy(total[:], wl[0:1, 15:16]).then_inc(work_ready, 1)
            done(vec.tensor_tensor(wl[:, 16:17], wl[:, 14:15], wl[:, 13:14], ALU.add))
            shift = float(1 << TBITS)
            done(vec.scalar_tensor_tensor(out=wl[:, 17:18], in0=wl[:, 14:15], scalar=-float(G), in1=wl[:, 11:12], op0=ALU.mult, op1=ALU.add))
            done(vec.tensor_scalar(wl[:, 17:18], wl[:, 17:18], -float(NOWHERE), shift, ALU.add, ALU.mult))
            done(vec.tensor_tensor(wl[:, 17:18], wl[:, 17:18], rowid[:], ALU.add))
            done(vec.memset(wl[:, 18:19], G * shift))
            for c in range(WORK // 512):
                if c:
                    dve.wait_ge(items_kept, c)
                q = Sf[:, 0:512]
                done(vec.tensor_scalar(q, iota512, 512.0 * c, None, ALU.add))
                done(vec.tensor_scalar(Tf, q, wl[:, 14:15], None, ALU.is_ge))
                done(vec.scalar_tensor_tensor(out=Vf, in0=q, scalar=wl[:, 16:17], in1=Tf, op0=ALU.is_lt, op1=ALU.mult))
                vec.tensor_tensor(Sf[:, 512:1024], Vf, q, ALU.mult).then_inc(cover_ready, 1)
                dve.wait_ge(items_ready, c + 1)
                vec.tensor_scalar(work[:, 512 * c:512 * c + 512], PS[0:1, 5 * 512:6 * 512], NOWHERE * shift, None,
                                  ALU.add).then_inc(items_kept, 1)
            def hot(b, u, j):
                dve.wait_ge(hots_used[b], OPEN + u)
                vec.tensor_tensor(hot_lo[b], dlo[:, ds(j, DB)].unsqueeze(2).broadcast_to([P, DB, P]),
                                  colid_b[:].unsqueeze(1).broadcast_to([P, DB, P]), ALU.is_equal)
                vec.tensor_tensor(hot_hi[b][:, :, 0:NT], dhi[:, ds(j, DB)].unsqueeze(2).broadcast_to([P, DB, NT]),
                                  colid_b[:, 0:NT].unsqueeze(1).broadcast_to([P, DB, NT]), ALU.is_equal).then_inc(hots[b], 1)
            with dve.Fori(0, BATCHES // 2) as i:
                for b in range(2):
                    hot(b, i, (2 * i + b) * DB)
            dve.wait_ge(degrees, 1)
            vec.tensor_scalar(lnbias[:], banks(6, NT), 1.0, None, ALU.add).then_inc(to_root, 1)

            def stats(t):
                for h in range(2):
                    ins = vec.bn_stats(bn[:, ds(t, 1), h, :].rearrange("p a c -> p (a c)"),
                                       acc[:, ds(t, 1), h * (D // 2):(h + 1) * (D // 2)].rearrange("p a c -> p (a c)"))
                return ins

            def aggregate():
                for t in range(NT):
                    ins = vec.bn_aggr(mv[:, t, :], bn[:, t, :, :].rearrange("p a c -> p (a c)"))
                done(ins)
                vec.tensor_scalar(lnscale[:], mv[:, :, 1], EPS, None, ALU.add).then_inc(to_root, 1)

            for k in range(NT // XC):
                dve.wait_ge(x_in[k], 16 if k < NT // XC - 1 else 32)
                for t in range(XC * k, XC * k + XC):
                    ins = stats(t)
            done(ins)
            aggregate()
            dve.wait_ge(rooted, 1)
            done(vec.reciprocal(dinv[:], dinv[:]))
            dve.wait_ge(rooted, 2)
            done(vec.reciprocal(rstd[:], rstd[:]))
            done(vec.tensor_tensor(lnscale[:], rstd[:], dinv[:], ALU.mult))
            vec.scalar_tensor_tensor(out=lnbias[:], in0=mv[:, :, 0], scalar=-1.0, in1=lnscale[:],
                                     op0=ALU.mult, op1=ALU.mult).then_inc(ln_ready, 1)

            def place(l, r, j, t):
                vec.tensor_scalar(dloc[:, r, :], dstF[:, ds(j, G)], tbase[:, ds(t, 1)], None,
                                  ALU.subtract).then_inc(local[l], 1)

            def select(l, r, q):
                place(l, r, *item(dve, q))
                dve.wait_ge(steps[l], G * q + G)
                dve.wait_ge(local[l], q + 1)
                for s in range(G):
                    ins = vec.tensor_scalar(S[:, r, s, :], colid[:], dloc[:, r, s:s + 1], None, ALU.is_equal)
                ins.then_inc(masked[l], 1)

            def raise_max(l, r, q, t):
                k = CH * q
                a = cand[:, r, :]
                T = logits[r % 2]
                Tf = T.rearrange(flat)
                dve.wait_ge(v_ready[l], q + 1)
                dve.wait_ge(p_ready[l], q + 1)
                vec.tensor_tensor(T, V[:], adrow[:, ds(t * P, P)].unsqueeze(1).broadcast_to([P, G, P]),
                                  ALU.add).then_inc(chain[l], 1)
                dve.wait_ge(u_ready[l], q + 1)
                vec.tensor_reduce(a[:, 0:1], banks(4 + r % 2), AX.X, ALU.max).then_inc(chain[l], 1)
                dve.wait_ge(chain[l], k + 2)
                vec.scalar_tensor_tensor(out=top[:, ds(t, 1)], in0=a[:, 0:1], scalar=adT[:, ds(t, 1)], in1=top[:, ds(t, 1)],
                                         op0=ALU.add, op1=ALU.max).then_inc(chain[l], 1)
                dve.wait_ge(chain[l], k + 3)
                vec.scalar_tensor_tensor(out=a[:, 1:2], in0=top[:, ds(t, 1)], scalar=SLOPE, in1=top[:, ds(t, 1)],
                                         op0=ALU.mult, op1=ALU.max).then_inc(chain[l], 1)
                dve.wait_ge(chain[l], k + 4)
                vec.tensor_scalar(diag[:, r % 2, :], ident[:], a[:, 1:2], None, ALU.mult).then_inc(chain[l], 1)
                vec.tensor_tensor(a[:, 2:3], mT[:, ds(t, 1)], a[:, 1:2], ALU.subtract).then_inc(chain[l], 1)
                vec.scalar_tensor_tensor(out=Tf, in0=Tf, scalar=SLOPE, in1=Tf, op0=ALU.mult, op1=ALU.max).then_inc(chain[l], 1)
                dve.wait_ge(chain[l], k + 6)
                vec.tensor_scalar(mT[:, ds(t, 1)], a[:, 1:2], 1.0, None, ALU.mult).then_inc(chain[l], 1)

            def less_max(l, r, q):
                dve.wait_ge(chain[l], CH * q + 8)
                dve.wait_ge(m_wide[l], q + 1)
                vec.tensor_tensor(logits[r % 2], logits[r % 2], banks(6 + r % 2, P).unsqueeze(1).broadcast_to([P, G, P]),
                                  ALU.subtract).then_inc(chain[l], 1)

            def evacuate(l, r, q, t):
                b = BANKS[l]
                dve.wait_ge(steps[l], STEPS0[l] + G * q + G)
                dve.wait_ge(evac[l], q + b)
                if l < 2:
                    ins = vec.tensor_tensor(tile(acc, t, D), tile(acc, t, D), banks(2 * (r % b), D), ALU.add)
                else:
                    dve.wait_ge(alpha_ready[l], q + 1)
                    ins = vec.scalar_tensor_tensor(out=tile(acc, t, EXT), in0=tile(acc, t, EXT), scalar=cand[:, r, 3:4],
                                                   in1=banks(2 * (r % b), EXT), op0=ALU.mult, op1=ALU.add)
                ins.then_inc(evac[l], 1)

            def agg(l):
                k = (0, 1, 3, 4)[l]
                if l >= 2:
                    def ad_to_diag(b, u, t):
                        dve.wait_ge(ad_wide[b], OPEN + at_ad(l, b, u))
                        vec.tensor_scalar(diag[:, b, :], ident[:], adT[:, ds(t, 1)], None, ALU.mult).then_inc(ad_diag[b], 1)
                    pairs(dve, ad_to_diag)
                    dve.wait_ge(ad_kept[0], OPEN + at_ad(l, 0, HALF) + 1)
                    dve.wait_ge(ad_kept[1], OPEN + at_ad(l, 1, HALF))
                dve.wait_ge(stored[0], 16 * at(k, 0, HALF) + 16)
                dve.wait_ge(stored[1], 16 * at(k, 1, HALF))
                n = rounds(dve, l)
                if l < 2:
                    select(l, 0, 0)
                    select(l, 1, 1)
                    with dve.Fori(0, n) as i:
                        for r in range(3):
                            select(l, (r + 2) % 3, 3 * i + r + 2)
                            evacuate(l, r, 3 * i + r, item(dve, 3 * i + r)[1])
                else:
                    for r in range(4):
                        place(l, r, *item(dve, r))
                    for r in range(3):
                        raise_max(l, r, r, item(dve, r)[1])
                        less_max(l, r, r)
                    place(l, 0, *item(dve, 4))
                    with dve.Fori(0, n) as i:
                        tiles = {0: item(dve, 4 * i)[1]}
                        for r in range(4):
                            q = 4 * i + r
                            evacuate(l, r, q, tiles[r])
                            if r < 2:
                                tiles[r + 3] = item(dve, q + 3)[1]
                            raise_max(l, (r + 3) % 4, q + 3, tiles[r + 3])
                            j, tiles[r + 5] = item(dve, q + 5)
                            place(l, (r + 1) % 4, j, tiles[r + 5])
                            if r < 2:
                                tiles[r + 1] = item(dve, q + 1)[1]
                            less_max(l, (r + 3) % 4, q + 3)
                dve.wait_ge(evac[l], BANKS[l] + RING[l] * n)
                dve.sem_inc(agg_done[l], 1)

            def extend(k, l):
                dve.wait_ge(w_in[k], 16)
                dve.wait_ge(att_in[k], 32)
                for c in range(KC):
                    for m in range(2):
                        done(vec.tensor_tensor_reduce(out=adrow[:, 0:D], in0=wbuf[:, k, c, 0:D], in1=attB[:, m, :],
                                                      scale=1.0, scalar=0.0, op0=ALU.mult, op1=ALU.add,
                                                      accum_out=wbuf[:, k, c, D + m:D + m + 1]))
                dve.sem_inc(ext_ready[k], 1)

            def linear(l):
                if l == 1:
                    extend(0, 2)
                if l != 2:
                    dve.wait_ge(pool_done[l if l < 2 else 2], 1)
                bias = {0: 0, 1: 1, 3: 2}.get(l)
                if bias is not None:
                    dve.wait_ge(bias_in[bias], 16)
                if l == 3:
                    done(vec.reciprocal(rden[:], acc[:, :, ONE]))

                def pre(b, u, t):
                    if l == 3:
                        dve.wait_ge(z_ready[b], OPEN + at(3, b, u))
                        vec.scalar_tensor_tensor(out=ybuf[b], in0=tile(acc, t, D), scalar=rden[:, ds(t, 1)], in1=bB[:],
                                                 op0=ALU.mult, op1=ALU.add).then_inc(z_pre[b], 1)

                def post(b, u, t):
                    dve.wait_ge(multiplied[b], OPEN + at(l, b, u) + 1)
                    psum = banks(2 * b, EXT)
                    if l < 2:
                        if l == 0:
                            dve.wait_ge(post_act[b], OPEN + at_act(0, b, u))
                        ins = vec.scalar_tensor_tensor(out=ybuf[b], in0=psum[:, 0:D], scalar=dinv[:, ds(t, 1)], in1=bB[:],
                                                       op0=ALU.mult, op1=ALU.add)
                        if l == 0:
                            ins.then_inc(post_dve[b], 1)
                            return
                        ins.then_inc(post_step[b], 1)
                        dve.wait_ge(post_step[b], 2 * at_step(1, b, u) + 1)
                        dve.wait_ge(xr_in[b], 16 * u + 16)
                        vec.tensor_tensor(tile(acc, t, D), ybuf[b], xin[b], ALU.add).then_inc(post_step[b], 1)
                        dve.wait_ge(post_step[b], 2 * at_step(1, b, u) + 2)
                        stats(t).then_inc(post_dve[b], 1)
                        return
                    a = c2[:, b, :]
                    vec.tensor_copy(a, psum[:, D:D + 2]).then_inc(post_step[b], 1)
                    dve.wait_ge(post_step[b], 2 * at_step(l, b, u) + 1)
                    vec.tensor_scalar(acc[:, ds(t, 1), ASRC], a[:, 0:1], 1.0, None, ALU.mult)
                    vec.tensor_scalar(adT[:, ds(t, 1)], a[:, 1:2], 1.0, None, ALU.mult)
                    vec.tensor_tensor(top[:, ds(t, 1)], a[:, 0:1], a[:, 1:2], ALU.add).then_inc(post_step[b], 1)
                    dve.wait_ge(post_step[b], 2 * at_step(l, b, u) + 2)
                    vec.scalar_tensor_tensor(out=mT[:, ds(t, 1)], in0=top[:, ds(t, 1)], scalar=SLOPE, in1=top[:, ds(t, 1)],
                                             op0=ALU.mult, op1=ALU.max).then_inc(post_dve[b], 1)

                if l >= 2:
                    done(vec.memset(acc[:, :, ONE], 1.0))
                pre(0, 0, 0)
                pre(1, 0, 1)
                with dve.Fori(0, HALF - 1) as i:
                    for b in range(2):
                        pre(b, i + 1, 2 * i + b + 2)
                        post(b, i, 2 * i + b)
                pre(0, HALF, NT - 1)
                post(0, HALF - 1, NT - 3)
                post(1, HALF - 1, NT - 2)
                post(0, HALF, NT - 1)
                if l == 1:
                    dve.wait_ge(post_dve[0], OPEN + at(1, 0, HALF) + 1)
                    aggregate()
                    dve.wait_ge(rooted, 3)
                    done(vec.reciprocal(rstd[:], rstd[:]))
                    done(vec.tensor_copy(lnscale[:], rstd[:]))
                    vec.scalar_tensor_tensor(out=lnbias[:], in0=mv[:, :, 0], scalar=-1.0, in1=rstd[:],
                                             op0=ALU.mult, op1=ALU.mult).then_inc(ln_ready, 1)
                if l == 2:
                    dve.wait_ge(post_dve[0], OPEN + at(2, 0, HALF) + 1)
                    extend(1, 3)
                if l == 3:
                    dve.wait_ge(post_dve[0], OPEN + at(3, 0, HALF) + 1)

            agg(0)
            linear(0)
            agg(1)
            linear(1)
            linear(2)
            agg(2)
            linear(3)
            agg(3)
            dve.wait_ge(pool_done[3], 1)
            dve.wait_ge(bias_in[3], 16)
            done(vec.reciprocal(rden[:], acc[:, :, ONE]))

            def final(b, u, t):
                dve.wait_ge(out_stored[b], OPEN + 16 * u)
                vec.scalar_tensor_tensor(out=ybuf[b], in0=tile(acc, t, D), scalar=rden[:, ds(t, 1)], in1=bB[:],
                                         op0=ALU.mult, op1=ALU.add).then_inc(fin_step[b], 1)
                dve.wait_ge(fin_step[b], u + 1)
                dve.wait_ge(x1r_in[b], 16 * u + 16)
                vec.tensor_tensor(ybuf[b], ybuf[b], xin[b], ALU.add).then_inc(fin[b], 1)
            pairs(dve, final)

        @block.tensor
        def _(pe):
            mm = nc.tensor.matmul
            open_up(pe, "pe")
            pe.wait_ge(prep, 4)
            pe.wait_ge(edges_f, 2)
            for k in range(2):
                for c in range(EB):
                    ins = nc.tensor.transpose(banks(k)[:, P * c:P * c + P], eflt[k][:, P * c:P * c + P], ident[:])
                ins.then_inc(blocks_turned, 1)
            pe.wait_ge(spans_diag, 1)
            for k in range(2):
                for c in range(EB):
                    o = P * (EB * k + c)
                    ins = mm(banks(2 + k)[:, P * c:P * c + P], ones[:], Sf[:, o:o + P], start=True, stop=True)
                ins.then_inc(spans_wide, 1)
            pe.wait_ge(counts_ready, 1)
            mm(banks(4)[:, 0:1], earlier, wl[:, 13:14], start=True, stop=True)
            mm(banks(4)[:, 1:2], ones[:], wl[:, 13:14], start=True, stop=True).then_inc(offsets_ready, 1)
            for c in range(WORK // 512):
                pe.wait_ge(cover_ready, c + 1)
                o = PS[0:1, 5 * 512:6 * 512]
                mm(o, wl[:, 17:18], Vf, start=True, stop=False)
                mm(o, wl[:, 18:19], Sf[:, 512:1024], start=False, stop=True).then_inc(items_ready, 1)

            def turn_w(k):
                pe.wait_ge(wnat_in, 16 * KC * (1 + k // KC))
                if k >= 2:
                    pe.wait_ge(wt_kept, k - 1)
                for c in range(KC):
                    ins = nc.tensor.transpose(banks(2 * (k % 2), D)[:, P * c:P * c + P], wnat[k % KC][:, P * c:P * c + P], ident[:])
                ins.then_inc(wnat_turned, 1)
            pe.wait_ge(items_kept, WORK // 512)
            for k in range(KC):
                turn_w(k)

            mm(banks(6, NT), zero_b[:], colid_b[:, 0:NT], start=True, stop=False)
            with pe.Fori(0, BATCHES // 2) as i:
                for b in range(2):
                    pe.wait_ge(hots[b], i + 1)
                    for k in range(DB):
                        ins = mm(banks(6, NT), hot_lo[b][:, k, :], hot_hi[b][:, k, 0:NT], start=False, stop=False)
                    ins.then_inc(hots_used[b], 1)
            mm(banks(6, NT), zero_b[:], colid_b[:, 0:NT], start=False, stop=True).then_inc(degrees, 1)
            for k in range(KC, 2 * KC):
                turn_w(k)
            pe.wait_ge(wt_kept, 2 * KC)

            def product(l, r, s):
                width = D if l < 2 else EXT
                b = 2 * (r % BANKS[l])
                mm(banks(b), sel[r][:, s, :], rows[r][:, s, 0:512], start=(s == 0), stop=(s == G - 1))
                mm(banks(b + 1, width - 512), sel[r][:, s, :], rows[r][:, s, 512:width],
                   start=(s == 0), stop=(s == G - 1)).then_inc(steps[l], 1)

            def turn_v(l, r, q):
                pe.wait_ge(v_ready[l], q + 1)
                for s in range(G):
                    ins = nc.tensor.transpose(banks(4 + r % 2)[:, P * s:P * s + P], V[:, s, :], ident[:])
                ins.then_inc(u_ready[l], 1)

            def widen_m(l, r, q):
                pe.wait_ge(chain[l], CH * q + 5)
                mm(banks(6 + r % 2, P), ones[:], diag[:, r % 2, :], start=True, stop=True).then_inc(m_wide[l], 1)

            def agg(l):
                if l >= 2:
                    def widen_ad(b, u, t):
                        pe.wait_ge(ad_diag[b], at_ad(l, b, u) + 1)
                        pe.wait_ge(ad_kept[b], OPEN + at_ad(l, b, u))
                        mm(banks(6 + b, P), ones[:], diag[:, b, :], start=True, stop=True).then_inc(ad_wide[b], 1)
                    pairs(pe, widen_ad)
                    for q in range(2):
                        turn_v(l, q, q)
                        widen_m(l, q, q)
                n = rounds(pe, l)
                with pe.Fori(0, n) as i:
                    for r in range(RING[l]):
                        q = RING[l] * i + r
                        if l < 2:
                            pe.wait_ge(masked[l], q + 1)
                        else:
                            pe.wait_ge(p_ready[l], 2 + q + 1)
                        pe.wait_ge(evac[l], q + 1)
                        pe.wait_ge(gathered[l][r], 16 * G * i + 16 * G)
                        product(l, r, 0)
                        if l >= 2:
                            turn_v(l, r, q + 2)
                        product(l, r, 1)
                        product(l, r, 2)
                        product(l, r, 3)
                        if l >= 2:
                            widen_m(l, r, q + 2)
                if l >= 2:
                    turn_v(l, 0, 4 * n + 2)
                    widen_m(l, 0, 4 * n + 2)

            def linear(l):
                width = D if l < 2 else EXT

                def turn_z(b, u):
                    pe.wait_ge(z_ready[b], OPEN + at(l, b, u) + 1)
                    pe.wait_ge(zT_ready[b], OPEN + at(l, b, u))
                    for c in range(KC):
                        ins = nc.tensor.transpose(banks(4 + 2 * b, D)[:, P * c:P * c + P], zst[b][:, P * c:P * c + P], ident[:])
                    ins.then_inc(turned[b], 1)

                def multiply(b, u):
                    pe.wait_ge(zT_ready[b], OPEN + at(l, b, u) + 1)
                    pe.wait_ge(post_dve[b], OPEN + at(l, b, u))
                    if l >= 2:
                        pe.wait_ge(post_act[b], OPEN + at_act(l, b, u))
                    for c in range(KC):
                        z = zT[b][:, P * c:P * c + P]
                        mm(banks(2 * b), z, wbuf[:, l % 2, c, 0:512], start=(c == 0), stop=(c == KC - 1))
                        ins = mm(banks(2 * b + 1, width - 512), z, wbuf[:, l % 2, c, 512:width],
                                 start=(c == 0), stop=(c == KC - 1))
                    ins.then_inc(multiplied[b], 1)

                if l >= 2:
                    pe.wait_ge(ext_ready[l - 2], 1)
                turn_z(0, 0)
                with pe.Fori(0, HALF) as i:
                    for b in range(2):
                        turn_z(1 - b, i + b)
                        multiply(b, i)
                multiply(0, HALF)

            agg(0)
            linear(0)
            agg(1)
            linear(1)
            linear(2)
            agg(2)
            linear(3)
            agg(3)


def kernel(x, src, dst, L0_gnn_W1, L0_gnn_b1, L0_gnn_W2, L0_gnn_b2, L1_gnn_W1, L1_gnn_att_src1, L1_gnn_att_dst1,
           L1_gnn_b1, L1_gnn_W2, L1_gnn_att_src2, L1_gnn_att_dst2, L1_gnn_b2):
    import numpy as np
    import concourse.bacc as bacc
    from concourse.bass_utils import run_bass_kernel_spmd

    given = {
        "x": x, "src": src, "dst": dst,
        "W1": L0_gnn_W1, "b1": L0_gnn_b1, "W2": L0_gnn_W2, "b2": L0_gnn_b2,
        "Wg1": L1_gnn_W1, "as1": L1_gnn_att_src1, "ad1": L1_gnn_att_dst1, "bg1": L1_gnn_b1,
        "Wg2": L1_gnn_W2, "as2": L1_gnn_att_src2, "ad2": L1_gnn_att_dst2, "bg2": L1_gnn_b2,
    }
    nc = bacc.Bacc("TRN2", target_bir_lowering=False, num_devices=1)
    arrays = {f"in_{k}": np.ascontiguousarray(v) for k, v in given.items()}
    args = [nc.dram_tensor(k, a.shape, mybir.dt.from_np(a.dtype), kind="ExternalInput").ap() for k, a in arrays.items()]
    out = nc.dram_tensor("out", arrays["in_x"].shape, F32, kind="ExternalOutput").ap()
    build(nc, *args, out)
    r = run_bass_kernel_spmd(nc, [arrays], core_ids=[0])
    return r.results[0]["out"]
```

```python
from contextlib import ExitStack

import concourse.bass as bass
from concourse import mybir

P = 128
ALU = mybir.AluOpType
ACT = mybir.ActivationFunctionType
AX = mybir.AxisListType
F32 = mybir.dt.float32
I32 = mybir.dt.int32
F32R = mybir.dt.float32r
BF16 = mybir.dt.bfloat16
ds = bass.ds

SLOPE = 0.2
EPS = 1e-5
FAR = -1.0e30
G = 4
RING = (3, 3, 4, 4)
OPEN = 1
CH = 9
TBITS = 5


def build(nc, x, src, dst, W1, b1, W2, b2, Wg1, as1, ad1, bg1, Wg2, as2, ad2, bg2, out):
    N, D = x.shape
    E = src.shape[0]
    NT = -(-N // P)
    LAST = N - (NT - 1) * P
    HALF = NT // 2
    EIGHTHS = NT // 8
    KC = D // P
    ROW = D + 4
    ONE, ASRC, EXT = D, D + 1, D + 2
    FULL, REST = E // P, E % P
    COLS = FULL + 1
    EB = -(-(COLS + 2 * G) // P)
    PAD = NT * P - 1
    NOWHERE = COLS + 1
    BIG = EB * P
    WORK = -(-(NT * -(-COLS // G) + 2 * max(RING) + 1) // 512) * 512
    DB = 14
    BATCHES = (COLS + 1) // DB
    XC = 5
    assert 0 < REST and N % P and NT == 2 * HALF + 1 and BATCHES * DB == COLS + 1 and NT < 1 << TBITS
    assert NT == 8 * EIGHTHS + 1 and G == 4
    assert 8 * (KC + 4) < FULL // G and NT % XC == 0 and BATCHES % 2 == 0

    with ExitStack() as ctx:
        def sb(name, shape, dt=F32):
            return ctx.enter_context(nc.sbuf_tensor(name, shape, dt))

        def sem(name):
            return ctx.enter_context(nc.semaphore(name))

        def sems(name, n):
            return [sem(f"{name}_{k}") for k in range(n)]

        table = nc.dram_tensor("table", [NT * P, ROW], F32)
        x1_dram = nc.dram_tensor("x1_dram", [NT * P, D], F32)
        w2t_dram = nc.dram_tensor("w2t_dram", [P, KC, D], F32)

        acc = sb("acc", [P, NT, ROW])
        wbuf_at = -(-nc.sbuf_base // 32) * 32
        wbuf = sb("wbuf", [P, 2, KC, EXT])
        ring_at = -(-nc.sbuf_base // 32) * 32
        ring = sb("ring", [P, 3, G, ROW])
        wr = nc.alloc_sbuf_tensor_at("wr", [P, 2, KC, EXT], F32R, offset=wbuf_at)
        zr = nc.alloc_sbuf_tensor_at("zr", [P, 2, 2, D], F32R, offset=ring_at)
        adrow = sb("adrow", [P, NT * P])
        S = sb("S", [P, 3, G, P])
        V = sb("V", [P, G, P])
        T = sb("T", [P, G, P])
        diag = sb("diag", [P, 2, P])
        cand = sb("cand", [P, 4, 4])
        colid_b = sb("colid_b", [P, P], BF16)
        zero_b = sb("zero_b", [P, P], BF16)
        bB = sb("bB", [P, D])
        attB = sb("attB", [P, 2, D])
        work = sb("work", [1, WORK], I32)
        total = sb("total", [1, 1], I32)
        srcI = sb("srcI", [P, EB * P], I32)
        dstF = sb("dstF", [P, EB * P])
        idx = sb("idx", [P, 4, G], I32)
        dloc = sb("dloc", [P, 4, G])
        ident = sb("ident", [P, P])
        ones = sb("ones", [P, P])
        colid = sb("colid", [P, P])
        rowid = sb("rowid", [P, 1])
        tbase = sb("tbase", [P, NT])
        dinv, adT, top, mT, rden, lnscale, lnbias, rstd = (
            sb(name, [P, NT]) for name in ("dinv", "adT", "top", "mT", "rden", "lnscale", "lnbias", "rstd"))
        bn = sb("bn", [P, NT, 2, 6])
        mv = sb("mv", [P, NT, 2])
        c2 = sb("c2", [P, 2, 2])
        wl = sb("wl", [P, 24])
        wli = sb("wli", [P, 2], I32)
        PS = ctx.enter_context(nc.psum_tensor("PS", [P, 8 * 512], F32))

        def banks(k, n=512):
            return PS[:, 512 * k:512 * k + n]

        zst = [ring[:, 1, b, 0:D] for b in range(2)]
        xin = [ring[:, 1, 2 + b, 0:D] for b in range(2)]
        ybuf = [ring[:, 2, b, 0:D] for b in range(2)]
        waiting = [adrow[:, EXT * c:EXT * (c + 1)] for c in range(4)] + [ring[:, 2, c - 2, 0:EXT] for c in range(4, KC)]
        ring_flat = ring[:].rearrange("p r g c -> p (r g c)")
        whole = XC * D
        x1_parts = [[(wbuf[:, 1, :, :].rearrange("p a b -> p (a b)")[:, 0:whole], 0, XC)],
                    [(ring_flat[:, 0:whole], XC, XC)],
                    [(ring_flat[:, whole:2 * whole], 2 * XC, XC)],
                    [(wbuf[:, 0, :, :].rearrange("p a b -> p (a b)")[:, 0:whole], 3 * XC, XC)],
                    [(adrow[:, 0:whole - D], 4 * XC, XC - 1), (ring_flat[:, 2 * whole:2 * whole + D], 5 * XC - 1, 1)]]
        wnat = [ring[:, c // G, c % G, 0:D] for c in range(KC)]
        eint = [ring[:, 2, k, 0:EB * P].bitcast(I32) for k in range(2)]
        eflt = [ring[:, 2, 2 + k, 0:EB * P] for k in range(2)]
        o = 0
        hot_lo, hot_hi = [], []
        for b in range(2):
            hot_lo.append(adrow[:, o:o + DB * P // 2].bitcast(BF16).rearrange("p (k e) -> p k e", k=DB))
            o += DB * P // 2
        for b in range(2):
            hot_hi.append(adrow[:, o:o + DB * 16].bitcast(BF16).rearrange("p (k e) -> p k e", k=DB))
            o += DB * 16
        iota512 = adrow[:, o:o + 512]
        dlo = bB[:, 0:EB * P // 2].bitcast(BF16)
        dhi = attB[:, 0, 0:EB * P // 2].bitcast(BF16)
        dint = attB[:, 1, 0:EB * P].bitcast(I32)
        earlier = diag[:, 0, :]
        flat = "p a b -> p (a b)"
        Vf, Tf = V[:].rearrange(flat), T[:].rearrange(flat)
        covers = [(Vf, S[:, 1, :, :].rearrange(flat)), (S[:, 2, :, :].rearrange(flat), attB[:, 0, EB * P // 2:EB * P // 2 + 512])]
        spare = wbuf[:, 0, :, :].rearrange(flat)
        def carve(o, n):
            return spare[:, o:o + n * G].rearrange("p (a b) -> p a b", a=G)
        rows = [ring[:, r, :, :] for r in range(3)] + [carve(0, ROW)]
        sel = [S[:, r, :, :] for r in range(3)] + [carve(G * ROW, P)]
        logits = [T[:], carve(G * (ROW + P), P)]
        o = G * (ROW + 2 * P)
        apart = spare[:, o:o + G * P // 2].bitcast(BF16).rearrange("p (a b) -> p a b", a=G)
        assert o + G * P // 2 <= KC * EXT
        Sf = S[:].rearrange("p r a b -> p (r a b)")

        padded = sem("padded")
        edges_in = sem("edges_in")
        consts = sem("consts")
        prep = sem("prep")
        edges_f = sem("edges_f")
        blocks_turned = sem("blocks_turned")
        spans_diag = sem("spans_diag")
        spans_wide = sem("spans_wide")
        counts_ready = sem("counts_ready")
        offsets_ready = sem("offsets_ready")
        cover_ready = sem("cover_ready")
        items_ready = sem("items_ready")
        items_kept = sem("items_kept")
        work_ready = sem("work_ready")
        x_in = sems("x_in", NT // XC)
        hots = sems("hots", 2)
        hots_used = sems("hots_used", 2)
        degrees = sem("degrees")
        to_root = sem("to_root")
        rooted = sem("rooted")
        ln_ready = sem("ln_ready")
        scaled = sem("scaled")
        wnat_in = sem("wnat_in")
        wnat_turned = sem("wnat_turned")
        wt_kept = sem("wt_kept")
        w2t_out = sem("w2t_out")
        weighed = sem("weighed")
        w2t_in = sem("w2t_in")
        split_hi = sem("split_hi")
        split_lo = sem("split_lo")
        w_in = sems("w_in", 2)
        att_in = sems("att_in", 2)
        ext_ready = sems("ext_ready", 2)
        bias_in = sems("bias_in", 4)
        stored = sems("stored", 2)
        gathered = [sems(f"gathered{l}", RING[l]) for l in range(4)]
        staged = [sem(f"staged{l}") for l in range(4)]
        idx_seen = sem("idx_seen")
        pool_done = [sem(f"pool_done{l}") for l in range(4)]
        local = [sem(f"local{l}") for l in range(4)]
        masked = [sem(f"masked{l}") for l in range(2)]
        steps = [sem(f"steps{l}") for l in range(4)]
        evac = [sem(f"evac{l}") for l in range(4)]
        agg_done = [sem(f"agg_done{l}") for l in range(4)]
        squared, v_ready, u_ready, chain, m_wide, p_ready, alpha_ready = (
            {l: sem(f"{name}{l}") for l in (2, 3)}
            for name in ("squared", "v_ready", "u_ready", "chain", "m_wide", "p_ready", "alpha_ready"))
        ad_diag = sems("ad_diag", 2)
        ad_wide = sems("ad_wide", 2)
        ad_kept = sems("ad_kept", 2)
        z_pre = sems("z_pre", 2)
        z_ready = sems("z_ready", 2)
        turned = sems("turned", 2)
        zT_ready = sems("zT_ready", 2)
        zT_low = sems("zT_low", 2)
        multiplied = sems("multiplied", 2)
        post_dve = sems("post_dve", 2)
        post_act = sems("post_act", 2)
        post_step = sems("post_step", 2)
        xr_in = sems("xr_in", 2)
        x1_in = sems("x1_in", NT // XC)
        scaled_out = sem("scaled_out")
        summed = sem("summed")
        out_stored = sem("out_stored")

        tab = table.rearrange("(t p) c -> p t c", p=P)
        x1t = x1_dram.rearrange("(t p) c -> p t c", p=P)
        x_t = x[0:(NT - 1) * P, :].rearrange("(t p) d -> p t d", p=P)
        out_t = out[0:(NT - 1) * P, :].rearrange("(t p) d -> p t d", p=P)

        def tile(a, t, n=None):
            v = a[:, ds(t, 1), :] if n is None else a[:, ds(t, 1), 0:n]
            return v.rearrange("p a c -> p (a c)")

        def wide(v):
            return v.rearrange("(o d) -> o d", o=1).broadcast_to([P, D])

        STEPS0 = [G * r for r in RING]
        BANKS = (3, 3, 2, 2)
        opened_by = {
            "pe": [(s, OPEN) for s in (*hots_used, *turned, *multiplied, *ad_wide)] + list(zip(steps, STEPS0)),
            "dve": [(s, OPEN) for s in (*post_dve, *zT_low)] + list(zip(evac, BANKS)),
            "act": [(s, OPEN) for s in (*z_ready, *post_act, *ad_kept)] + [(s, 2) for s in p_ready.values()],
        }
        def open_up(eng, group):
            for s, n in opened_by[group]:
                eng.sem_inc(s, n)

        def at(l, b, u):
            return l * (HALF + 1 - b) + u

        def at_act(l, b, u):
            return at(max(l - 1, 0), b, u)

        def at_step(l, b, u):
            return at(l - 1, b, u)

        def at_ad(l, b, u):
            return (l - 2) * (EIGHTHS + 1 - b) + u

        def rounds(eng, l):
            v = eng.value_load(total[0:1, 0:1], min_val=1, max_val=NT * -(-COLS // G))
            most = -(-NT * -(-COLS // G) // RING[l])
            if RING[l] == 4:
                return eng.snap((v + 3) >> 2).with_bounds(min_val=1, max_val=most)
            return eng.snap(((v + 2) * 21846) >> 16).with_bounds(min_val=1, max_val=most)

        def item(eng, q):
            v = eng.value_load(work[0:1, ds(q, 1)], min_val=0, max_val=((NOWHERE + 1) << TBITS) - 1)
            j = eng.snap(v >> TBITS).with_bounds(min_val=0, max_val=NOWHERE)
            t = eng.snap(v & ((1 << TBITS) - 1)).with_bounds(min_val=0, max_val=NT - 1)
            return j, t

        def raw_weights(l, c):
            return waiting[c] if l == 2 else wbuf[:, 1, c, 0:(D if l < 2 else EXT)]

        def pairs(eng, step):
            with eng.Fori(0, HALF) as i:
                for b in range(2):
                    step(b, i, 2 * i + b)
            step(0, HALF, NT - 1)

        def fours(eng, step):
            with eng.Fori(0, EIGHTHS) as i:
                for b in range(2):
                    step(b, i, 8 * i + 4 * b, 4)
            step(0, EIGHTHS, NT - 1, 1)

        block = ctx.enter_context(nc.Block())

        @block.sync
        def _(sp):
            sp.wait_ge(padded, 2)
            whole = FULL // P
            rest = FULL - whole * P
            for v, e in ((dst, eint[0]), (src, eint[1])):
                e = e.rearrange("p (k e) -> p k e", k=EB)
                sp.dma_start(e[:, 0:whole, :], v[0:whole * P * P].rearrange("(k p e) -> p k e", p=P, e=P)).then_inc(edges_in, 16)
                sp.dma_start(e[0:rest, whole, :], v[whole * P * P:FULL * P].rearrange("(p e) -> p e", e=P)).then_inc(edges_in, 16)
                sp.dma_start(e[rest:rest + 1, whole, 0:REST], v[FULL * P:E].rearrange("(p e) -> p e", p=1)).then_inc(edges_in, 16)
            for c in range(KC):
                sp.dma_start(wnat[c], W1[c * P:(c + 1) * P, :]).then_inc(wnat_in, 16)
            sp.wait_ge(padded, 3)
            for k in range(NT // XC):
                n = XC if k < NT // XC - 1 else XC - 1
                sp.dma_start(acc[:, XC * k:XC * k + n, 0:D], x_t[:, XC * k:XC * k + n, :]).then_inc(x_in[k], 16)
            sp.dma_start(acc[0:LAST, NT - 1, 0:D], x[(NT - 1) * P:N, :]).then_inc(x_in[NT // XC - 1], 16)
            sp.wait_ge(wnat_turned, KC)
            for c in range(KC):
                sp.dma_start(wnat[c], W2[c * P:(c + 1) * P, :]).then_inc(wnat_in, 16)

            sp.wait_ge(wt_kept, 2 * KC)
            sp.dma_start(w2t_dram[:, :, :], wbuf[:, 0, :, 0:D]).then_inc(w2t_out, 16)
            def store0(b, u, t):
                sp.wait_ge(scaled, t + 1)
                sp.dma_start(tile(tab, t), tile(acc, t)).then_inc(stored[b], 16)
            pairs(sp, store0)
            sp.wait_ge(degrees, 1)
            sp.dma_start(bB[:], wide(b1)).then_inc(bias_in[0], 16)

            def store_rows(l):
                def store(b, u, t):
                    sp.wait_ge(post_act[b], OPEN + at_act(l, b, u) + 1)
                    sp.dma_start(tile(tab, t), tile(acc, t)).then_inc(stored[b], 16)
                return store

            pairs(sp, store_rows(0))
            sp.dma_start(bB[:], wide(b2)).then_inc(bias_in[1], 16)
            sp.wait_ge(w2t_out, 16)
            for c in range(KC):
                sp.wait_ge(evac[1], BANKS[1] + 8 * (c + 1))
                sp.dma_start(wbuf[:, 1, c, 0:D], w2t_dram[:, c, :]).then_inc(w2t_in, 16)
            for c in range(4):
                sp.wait_ge(evac[1], BANKS[1] + 8 * (KC + c + 1))
                sp.dma_start(waiting[c][:, 0:D], Wg1[c * P:(c + 1) * P, :]).then_inc(w_in[0], 16)
            for k, a in enumerate((as1, ad1)):
                sp.dma_start(attB[:, k, :], wide(a)).then_inc(att_in[0], 16)

            sp.wait_ge(agg_done[1], 1)
            sp.wait_ge(pool_done[1], 1)
            for c in range(4, KC):
                sp.dma_start(waiting[c][:, 0:D], Wg1[c * P:(c + 1) * P, :]).then_inc(w_in[0], 16)

            def load_x(b, u, t):
                sp.wait_ge(post_dve[b], OPEN + at(1, b, u))
                sp.dma_start(xin[b], tile(x_t, t)).then_inc(xr_in[b], 16)

            def store_x1(b, u, t):
                sp.wait_ge(post_dve[b], OPEN + at(1, b, u) + 1)
                sp.dma_start(tile(x1t, t), tile(acc, t, D)).then_inc(stored[b], 16)

            load_x(0, 0, 0)
            load_x(1, 0, 1)
            with sp.Fori(0, HALF - 1) as i:
                for b in range(2):
                    store_x1(b, i, 2 * i + b)
                    load_x(b, i + 1, 2 * i + b + 2)
            store_x1(0, HALF - 1, NT - 3)
            sp.dma_start(xin[0][0:LAST, :], x[(NT - 1) * P:N, :]).then_inc(xr_in[0], 16)
            store_x1(1, HALF - 1, NT - 2)
            store_x1(0, HALF, NT - 1)
            sp.dma_start(bB[:], wide(bg1)).then_inc(bias_in[2], 16)
            sp.wait_ge(ext_ready[0], 1)
            for k, a in enumerate((as2, ad2)):
                sp.dma_start(attB[:, k, :], wide(a)).then_inc(att_in[1], 16)
            sp.wait_ge(split_lo, 3 * KC)
            for c in range(KC):
                sp.dma_start(waiting[c][:, 0:D], Wg2[c * P:(c + 1) * P, :]).then_inc(w_in[1], 16)
            sp.wait_ge(stored[0], 16 * at(2, 0, HALF) + 16)
            sp.wait_ge(stored[1], 16 * at(2, 1, HALF))
            pairs(sp, store_rows(2))
            pairs(sp, store_rows(3))
            sp.dma_start(bB[:], wide(bg2)).then_inc(bias_in[3], 16)

            def load_x1(k):
                for buf, t, m in x1_parts[k]:
                    sp.dma_start(buf.rearrange("p (t d) -> p t d", d=D), x1t[:, t:t + m, :]).then_inc(x1_in[k], 16)
            load_x1(0)
            sp.wait_ge(agg_done[3], 1)
            sp.wait_ge(pool_done[3], 1)
            sp.wait_ge(weighed, 2)
            for k in range(1, NT // XC):
                load_x1(k)
            for k in range(NT // XC):
                m = XC if k < NT // XC - 1 else XC - 1
                sp.wait_ge(summed, k + 1)
                sp.dma_start(out_t[:, XC * k:XC * k + m, :], acc[:, XC * k:XC * k + m, 0:D]).then_inc(out_stored, 16)
            sp.dma_start(out[(NT - 1) * P:N, :], acc[0:LAST, NT - 1, 0:D]).then_inc(out_stored, 16)
            sp.wait_ge(out_stored, 16 * (NT // XC + 1))

        @block.gpsimd
        def _(pool):
            nc.gpsimd.memset(eint[0], PAD).then_inc(padded, 1)
            nc.gpsimd.memset(eint[1], 0).then_inc(padded, 1)
            nc.gpsimd.memset(acc[:, NT - 1, :], 0.0).then_inc(padded, 1)
            for a, pattern, m in ((colid[:], [[1, P]], 0), (rowid[:], [[0, 1]], 1), (tbase[:], [[P, NT]], 0),
                                  (colid_b[:], [[1, P]], 0), (iota512, [[1, 512]], 0)):
                nc.gpsimd.iota(a, pattern=pattern, base=0, channel_multiplier=m,
                               allow_small_or_imprecise_dtypes=True).then_inc(consts, 1)
            nc.gpsimd.memset(acc[:, 0:NT - 1, D:ROW], 0.0).then_inc(consts, 1)
            pool.wait_ge(work_ready, 2)

            def gather(l, r, q, j):
                pool.wait_ge(steps[l], G * q + (G if l < 2 else 1))
                nc.gpsimd.tensor_copy(idx[:, r, :], srcI[:, ds(j, G)]).then_inc(staged[l], 1)
                pool.wait_ge(staged[l], q + 1)
                for s in range(G):
                    if l >= 2 and s:
                        pool.wait_ge(steps[l], G * q + s + 1)
                    if l >= 2 or s == 0:
                        nc.gpsimd.sem_inc(idx_seen, 1)
                    nc.gpsimd.indirect_dma_start(
                        out=rows[r][:, s, :], out_offset=None, in_=table[:, :],
                        in_offset=bass.IndirectOffsetOnAxis(ap=idx[:, r, s:s + 1], axis=0),
                    ).then_inc(gathered[l][r], 16)

            for l in range(4):
                k = (0, 1, 3, 4)[l]
                n = rounds(pool, l)
                pool.wait_ge(stored[0], 16 * at(k, 0, HALF) + 16)
                pool.wait_ge(stored[1], 16 * at(k, 1, HALF))
                if l == 0:
                    pool.wait_ge(wnat_turned, 2 * KC)
                if l == 2:
                    pool.wait_ge(ext_ready[1], 1)
                for r in range(RING[l]):
                    gather(l, r, r, item(pool, r)[0])
                with pool.Fori(0, n) as i:
                    for r in range(RING[l]):
                        q = RING[l] * (i + 1) + r
                        gather(l, r, q, item(pool, q)[0])
                for r in range(RING[l]):
                    pool.wait_ge(gathered[l][r], 16 * G * n + 16 * G)
                nc.gpsimd.sem_inc(pool_done[l], 1)

        @block.scalar
        def _(act):
            open_up(act, "act")
            def keep_wt(k):
                act.wait_ge(wnat_turned, k + 1)
                l, c = divmod(k, KC)
                nc.scalar.copy(wbuf[:, 1 - l, :, P * c:P * c + P],
                               banks(2 * (k % 2), D).rearrange("p (c f) -> p c f", f=P)).then_inc(wt_kept, 1)
            for k in range(2 * KC):
                keep_wt(k)
            act.wait_ge(to_root, 1)
            nc.scalar.activation(dinv[:], lnbias[:], ACT.Sqrt).then_inc(rooted, 1)
            act.wait_ge(to_root, 2)
            nc.scalar.activation(rstd[:], lnscale[:], ACT.Sqrt).then_inc(rooted, 1)
            act.wait_ge(ln_ready, 1)

            def scale0(b, u, t):
                nc.scalar.activation(tile(acc, t, D), tile(acc, t, D), ACT.Relu, bias=lnbias[:, ds(t, 1)],
                                     scale=lnscale[:, ds(t, 1)]).then_inc(scaled, 1)
            pairs(act, scale0)

            def far(l, r, u, q, first=False):
                act.wait_ge(local[l], q + 1)
                if not first:
                    act.wait_ge(v_ready[l], q)
                for s in range(G):
                    last = nc.scalar.activation(apart[:, s, :], colid[:], ACT.Square, scale=-1.0,
                                                bias=dloc[:, r, s:s + 1])
                last.then_inc(squared[l], 1)
                act.wait_ge(squared[l], q + 1)
                act.wait_ge(gathered[l][r], 16 * G * u + 16 * G)
                if not first:
                    act.wait_ge(chain[l], CH * q - CH + 1)
                    act.wait_ge(u_ready[l], q)
                for s in range(G):
                    last = nc.scalar.activation(V[:, s, :], apart[:, s, :], ACT.Identity, scale=FAR,
                                                bias=rows[r][:, s, ASRC:ASRC + 1])
                last.then_inc(v_ready[l], 1)

            def weigh(l, r, q):
                act.wait_ge(chain[l], CH * q + CH)
                act.wait_ge(steps[l], G * q + G)
                nc.scalar.activation(sel[r].rearrange(flat), logits[r % 2].rearrange(flat), ACT.Exp).then_inc(p_ready[l], 1)
                nc.scalar.activation(cand[:, r, 3:4], cand[:, r, 2:3], ACT.Exp).then_inc(alpha_ready[l], 1)

            def agg(l):
                if l < 2:
                    return
                def keep_ad(b, u, t, m):
                    act.wait_ge(ad_wide[b], OPEN + at_ad(l, b, u) + 1)
                    nc.scalar.copy(adrow[:, ds(t * P, m * P)], banks(6 + b, m * P)).then_inc(ad_kept[b], 1)
                fours(act, keep_ad)
                n = rounds(act, l)
                far(l, 0, 0, 0, first=True)
                far(l, 1, 0, 1)
                weigh(l, 0, 0)
                far(l, 2, 0, 2)
                weigh(l, 1, 1)
                with act.Fori(0, n) as i:
                    for r in range(4):
                        far(l, (r + 3) % 4, i + (r + 3) // 4, 4 * i + r + 3)
                        weigh(l, (r + 2) % 4, 4 * i + r + 2)
                act.wait_ge(p_ready[l], 4 * n + 4)
                nc.scalar.sem_inc(weighed, 1)

            def linear(l):
                width = D if l < 2 else EXT

                def z_stage(b, u, t):
                    if l == 3:
                        act.wait_ge(z_pre[b], u + 1)
                    act.wait_ge(turned[b], OPEN + at(l, b, u))
                    if l < 2:
                        ins = nc.scalar.copy(zst[b], tile(acc, t, D))
                    elif l == 2:
                        ins = nc.scalar.activation(zst[b], tile(acc, t, D), ACT.Relu, bias=lnbias[:, ds(t, 1)],
                                                   scale=lnscale[:, ds(t, 1)])
                    else:
                        ins = nc.scalar.activation(zst[b], ybuf[b], ACT.Relu)
                    ins.then_inc(z_ready[b], 1)

                def keep_zT(b, u, t):
                    act.wait_ge(turned[b], OPEN + at(l, b, u) + 1)
                    act.wait_ge(multiplied[b], OPEN + at(l, b, u))
                    nc.scalar.copy(zr[:, b, 0, :], banks(4 + 2 * b, D)).then_inc(zT_ready[b], 1)

                def post(b, u, t):
                    if l == 0:
                        act.wait_ge(post_dve[b], OPEN + at(0, b, u) + 1)
                        nc.scalar.activation(tile(acc, t, D), ybuf[b], ACT.Relu,
                                             scale=dinv[:, ds(t, 1)]).then_inc(post_act[b], 1)
                    elif l >= 2:
                        act.wait_ge(post_dve[b], OPEN + at(l, b, u) + 1)
                        nc.scalar.copy(tile(acc, t, D), banks(2 * b, D)).then_inc(post_act[b], 1)

                if l == 0:
                    act.wait_ge(wt_kept, 2 * KC)
                    act.wait_ge(w2t_out, 16)
                elif l < 3:
                    act.wait_ge(multiplied[0], OPEN + at(l, 0, 0))
                    act.wait_ge(multiplied[1], OPEN + at(l, 1, 0))
                if l == 1:
                    act.wait_ge(w2t_in, 16 * KC)
                if l >= 2:
                    act.wait_ge(ext_ready[l - 2], 1)
                if l == 3:
                    act.wait_ge(agg_done[2], 1)
                    act.wait_ge(pool_done[2], 1)
                for c in range(KC):
                    nc.scalar.copy(wr[:, 0, c, 0:width], raw_weights(l, c)).then_inc(split_hi, 1)
                if l == 2:
                    act.wait_ge(to_root, 3)
                    nc.scalar.activation(rstd[:], lnscale[:], ACT.Sqrt).then_inc(rooted, 1)
                    act.wait_ge(rooted, 3)
                    act.wait_ge(ln_ready, 2)
                    act.wait_ge(stored[0], 16 * at(2, 0, HALF) + 16)
                    act.wait_ge(stored[1], 16 * at(2, 1, HALF))
                else:
                    k = l if l < 2 else 2
                    act.wait_ge(agg_done[k], 1)
                    act.wait_ge(pool_done[k], 1)
                z_stage(0, 0, 0)
                z_stage(1, 0, 1)
                keep_zT(0, 0, 0)
                with act.Fori(0, HALF - 1) as i:
                    for b in range(2):
                        keep_zT(1 - b, i + b, 2 * i + b + 1)
                        z_stage(b, i + 1, 2 * i + b + 2)
                        post(b, i, 2 * i + b)
                keep_zT(1, HALF - 1, NT - 2)
                z_stage(0, HALF, NT - 1)
                post(0, HALF - 1, NT - 3)
                keep_zT(0, HALF, NT - 1)
                post(1, HALF - 1, NT - 2)
                post(0, HALF, NT - 1)
            agg(0)
            linear(0)
            agg(1)
            linear(1)
            linear(2)
            agg(2)
            linear(3)
            agg(3)

        @block.vector
        def _(dve):
            count = [0]

            def done(ins):
                count[0] += 1
                ins.then_inc(prep, 1)
                dve.wait_ge(prep, count[0])

            vec = nc.vector
            open_up(dve, "dve")
            dve.wait_ge(consts, 6)
            done(vec.tensor_scalar(ident[:], colid[:], rowid[:], None, ALU.is_equal))
            done(vec.memset(ones[:], 1.0))
            done(vec.tensor_scalar(earlier, colid[:], rowid[:], None, ALU.is_gt))
            done(vec.memset(zero_b[:], 0.0))
            dve.wait_ge(edges_in, 96)
            vec.tensor_copy(eflt[0], eint[0]).then_inc(edges_f, 1)
            vec.tensor_copy(eflt[1], eint[1]).then_inc(edges_f, 1)
            dve.wait_ge(edges_f, 2)
            e3 = eflt[0].rearrange("p (k e) -> p k e", k=EB)
            done(vec.tensor_reduce(wl[:, 0:EB], e3, AX.X, ALU.min))
            done(vec.tensor_reduce(wl[:, 4:4 + EB], e3, AX.X, ALU.max))
            for k in range(2 * EB):
                c = k if k < EB else 4 + k - EB
                ins = vec.tensor_scalar(Sf[:, P * k:P * k + P], ident[:], wl[:, c:c + 1], None, ALU.mult)
            ins.then_inc(spans_diag, 1)
            dve.wait_ge(blocks_turned, 2)
            done(vec.tensor_copy(dstF[:], banks(0)))
            vec.tensor_copy(srcI[:], banks(1)).then_inc(work_ready, 1)
            done(vec.tensor_copy(dint, dstF[:]))
            done(vec.tensor_scalar(eint[0], dint, P - 1, None, ALU.bitwise_and))
            done(vec.tensor_copy(dlo, eint[0]))
            done(vec.tensor_scalar(eint[0], dint, 7, None, ALU.logical_shift_right))
            done(vec.tensor_copy(dhi, eint[0]))
            done(vec.tensor_scalar(wl[:, 8:9], rowid[:], float(P), None, ALU.mult))
            done(vec.tensor_scalar(wl[:, 9:10], rowid[:], float(P), float(P - 1), ALU.mult, ALU.add))
            dve.wait_ge(spans_wide, 2)
            cov, tmp = Vf[:, 0:COLS], Tf[:, 0:COLS]
            done(vec.tensor_scalar(tmp, banks(3, COLS), wl[:, 8:9], None, ALU.is_ge))
            done(vec.scalar_tensor_tensor(out=cov, in0=banks(2, COLS), scalar=wl[:, 9:10], in1=tmp,
                                          op0=ALU.is_le, op1=ALU.mult))
            done(vec.scalar_tensor_tensor(out=tmp, in0=iota512[:, 0:COLS], scalar=1.0, in1=cov, op0=ALU.add, op1=ALU.mult))
            done(vec.tensor_reduce(wl[:, 10:11], tmp, AX.X, ALU.max))
            done(vec.scalar_tensor_tensor(out=tmp, in0=iota512[:, 0:COLS], scalar=-float(BIG), in1=cov, op0=ALU.add, op1=ALU.mult))
            done(vec.tensor_reduce(wl[:, 11:12], tmp, AX.X, ALU.min))
            done(vec.tensor_scalar(wl[:, 11:12], wl[:, 11:12], float(BIG), None, ALU.add))
            done(vec.tensor_tensor(wl[:, 12:13], wl[:, 10:11], wl[:, 11:12], ALU.subtract))
            done(vec.tensor_scalar(wl[:, 12:13], wl[:, 12:13], float(G - 1), 0.0, ALU.add, ALU.max))
            done(vec.tensor_copy(wli[:, 0:1], wl[:, 12:13]))
            done(vec.tensor_scalar(wli[:, 1:2], wli[:, 0:1], G.bit_length() - 1, None, ALU.logical_shift_right))
            vec.tensor_copy(wl[:, 13:14], wli[:, 1:2]).then_inc(counts_ready, 1)
            dve.wait_ge(offsets_ready, 1)
            done(vec.tensor_copy(wl[:, 14:16], banks(4, 2)))
            vec.tensor_copy(total[:], wl[0:1, 15:16]).then_inc(work_ready, 1)
            done(vec.tensor_tensor(wl[:, 16:17], wl[:, 14:15], wl[:, 13:14], ALU.add))
            shift = float(1 << TBITS)
            done(vec.scalar_tensor_tensor(out=wl[:, 17:18], in0=wl[:, 14:15], scalar=-float(G), in1=wl[:, 11:12], op0=ALU.mult, op1=ALU.add))
            done(vec.tensor_scalar(wl[:, 17:18], wl[:, 17:18], -float(NOWHERE), shift, ALU.add, ALU.mult))
            done(vec.tensor_tensor(wl[:, 17:18], wl[:, 17:18], rowid[:], ALU.add))
            done(vec.memset(wl[:, 18:19], G * shift))
            def keep_items(c):
                dve.wait_ge(items_ready, c + 1)
                vec.tensor_scalar(work[:, 512 * c:512 * c + 512], PS[0:1, 512 * (5 + 2 * (c % 2)):][:, 0:512],
                                  NOWHERE * shift, None, ALU.add).then_inc(items_kept, 1)

            for c in range(WORK // 512):
                q, (held, numbered) = Sf[:, 0:512], covers[c % 2]
                done(vec.tensor_scalar(q, iota512, 512.0 * c, None, ALU.add))
                done(vec.tensor_scalar(Tf, q, wl[:, 14:15], None, ALU.is_ge))
                done(vec.scalar_tensor_tensor(out=held, in0=q, scalar=wl[:, 16:17], in1=Tf, op0=ALU.is_lt, op1=ALU.mult))
                vec.tensor_tensor(numbered, held, q, ALU.mult).then_inc(cover_ready, 1)
                dve.wait_ge(cover_ready, c + 1)
                if c:
                    keep_items(c - 1)
            keep_items(WORK // 512 - 1)
            def hot(b, u, j):
                dve.wait_ge(hots_used[b], OPEN + u)
                vec.tensor_tensor(hot_lo[b], dlo[:, ds(j, DB)].unsqueeze(2).broadcast_to([P, DB, P]),
                                  colid_b[:].unsqueeze(1).broadcast_to([P, DB, P]), ALU.is_equal)
                vec.tensor_tensor(hot_hi[b][:, :, 0:NT], dhi[:, ds(j, DB)].unsqueeze(2).broadcast_to([P, DB, NT]),
                                  colid_b[:, 0:NT].unsqueeze(1).broadcast_to([P, DB, NT]), ALU.is_equal).then_inc(hots[b], 1)
            with dve.Fori(0, BATCHES // 2) as i:
                for b in range(2):
                    hot(b, i, (2 * i + b) * DB)
            dve.wait_ge(degrees, 1)
            vec.tensor_scalar(lnbias[:], banks(6, NT), 1.0, None, ALU.add).then_inc(to_root, 1)

            def stats(t):
                for h in range(2):
                    ins = vec.bn_stats(bn[:, ds(t, 1), h, :].rearrange("p a c -> p (a c)"),
                                       acc[:, ds(t, 1), h * (D // 2):(h + 1) * (D // 2)].rearrange("p a c -> p (a c)"))
                return ins

            def aggregate():
                for t in range(NT):
                    ins = vec.bn_aggr(mv[:, t, :], bn[:, t, :, :].rearrange("p a c -> p (a c)"))
                done(ins)
                vec.tensor_scalar(lnscale[:], mv[:, :, 1], EPS, None, ALU.add).then_inc(to_root, 1)

            for k in range(NT // XC):
                dve.wait_ge(x_in[k], 16 if k < NT // XC - 1 else 32)
                for t in range(XC * k, XC * k + XC):
                    ins = stats(t)
            done(ins)
            aggregate()
            dve.wait_ge(rooted, 1)
            done(vec.reciprocal(dinv[:], dinv[:]))
            dve.wait_ge(rooted, 2)
            done(vec.reciprocal(rstd[:], rstd[:]))
            done(vec.tensor_tensor(lnscale[:], rstd[:], dinv[:], ALU.mult))
            vec.scalar_tensor_tensor(out=lnbias[:], in0=mv[:, :, 0], scalar=-1.0, in1=lnscale[:],
                                     op0=ALU.mult, op1=ALU.mult).then_inc(ln_ready, 1)

            def place(l, r, j, t):
                vec.tensor_scalar(dloc[:, r, :], dstF[:, ds(j, G)], tbase[:, ds(t, 1)], None,
                                  ALU.subtract).then_inc(local[l], 1)

            def select(l, r, q):
                place(l, r, *item(dve, q))
                dve.wait_ge(steps[l], G * q + G)
                dve.wait_ge(local[l], q + 1)
                for s in range(G):
                    ins = vec.tensor_scalar(S[:, r, s, :], colid[:], dloc[:, r, s:s + 1], None, ALU.is_equal)
                ins.then_inc(masked[l], 1)

            def raise_max(l, r, q, t):
                k = CH * q
                a = cand[:, r, :]
                T = logits[r % 2]
                Tf = T.rearrange(flat)
                dve.wait_ge(v_ready[l], q + 1)
                dve.wait_ge(p_ready[l], q + 1)
                vec.tensor_tensor(T, V[:], adrow[:, ds(t * P, P)].unsqueeze(1).broadcast_to([P, G, P]),
                                  ALU.add).then_inc(chain[l], 1)
                dve.wait_ge(u_ready[l], q + 1)
                vec.tensor_reduce(a[:, 0:1], banks(4 + r % 2), AX.X, ALU.max).then_inc(chain[l], 1)
                dve.wait_ge(chain[l], k + 2)
                vec.scalar_tensor_tensor(out=top[:, ds(t, 1)], in0=a[:, 0:1], scalar=adT[:, ds(t, 1)], in1=top[:, ds(t, 1)],
                                         op0=ALU.add, op1=ALU.max).then_inc(chain[l], 1)
                dve.wait_ge(chain[l], k + 3)
                vec.scalar_tensor_tensor(out=a[:, 1:2], in0=top[:, ds(t, 1)], scalar=SLOPE, in1=top[:, ds(t, 1)],
                                         op0=ALU.mult, op1=ALU.max).then_inc(chain[l], 1)
                dve.wait_ge(chain[l], k + 4)
                vec.tensor_scalar(diag[:, r % 2, :], ident[:], a[:, 1:2], None, ALU.mult).then_inc(chain[l], 1)
                vec.tensor_tensor(a[:, 2:3], mT[:, ds(t, 1)], a[:, 1:2], ALU.subtract).then_inc(chain[l], 1)
                vec.scalar_tensor_tensor(out=Tf, in0=Tf, scalar=SLOPE, in1=Tf, op0=ALU.mult, op1=ALU.max).then_inc(chain[l], 1)
                dve.wait_ge(chain[l], k + 6)
                vec.tensor_scalar(mT[:, ds(t, 1)], a[:, 1:2], 1.0, None, ALU.mult).then_inc(chain[l], 1)

            def less_max(l, r, q):
                dve.wait_ge(chain[l], CH * q + 8)
                dve.wait_ge(m_wide[l], q + 1)
                vec.tensor_tensor(logits[r % 2], logits[r % 2], banks(6 + r % 2, P).unsqueeze(1).broadcast_to([P, G, P]),
                                  ALU.subtract).then_inc(chain[l], 1)

            def evacuate(l, r, q, t):
                b = BANKS[l]
                dve.wait_ge(steps[l], STEPS0[l] + G * q + G)
                dve.wait_ge(evac[l], q + b)
                if l < 2:
                    ins = vec.tensor_tensor(tile(acc, t, D), tile(acc, t, D), banks(2 * (r % b), D), ALU.add)
                else:
                    dve.wait_ge(alpha_ready[l], q + 1)
                    ins = vec.scalar_tensor_tensor(out=tile(acc, t, EXT), in0=tile(acc, t, EXT), scalar=cand[:, r, 3:4],
                                                   in1=banks(2 * (r % b), EXT), op0=ALU.mult, op1=ALU.add)
                ins.then_inc(evac[l], 1)

            def agg(l):
                k = (0, 1, 3, 4)[l]
                if l >= 2:
                    def ad_to_diag(b, u, t, m):
                        dve.wait_ge(ad_wide[b], OPEN + at_ad(l, b, u))
                        for k in range(m):
                            ins = vec.tensor_scalar(S[:, b, k, :], ident[:], adT[:, ds(t + k, 1)], None, ALU.mult)
                        ins.then_inc(ad_diag[b], 1)
                    fours(dve, ad_to_diag)
                    dve.wait_ge(ad_kept[0], OPEN + at_ad(l, 0, EIGHTHS) + 1)
                    dve.wait_ge(ad_kept[1], OPEN + at_ad(l, 1, EIGHTHS))
                n = rounds(dve, l)
                if l < 2:
                    select(l, 0, 0)
                    select(l, 1, 1)
                    dve.wait_ge(stored[0], 16 * at(k, 0, HALF) + 16)
                    dve.wait_ge(stored[1], 16 * at(k, 1, HALF))
                    with dve.Fori(0, n) as i:
                        for r in range(3):
                            select(l, (r + 2) % 3, 3 * i + r + 2)
                            evacuate(l, r, 3 * i + r, item(dve, 3 * i + r)[1])
                else:
                    for r in range(4):
                        place(l, r, *item(dve, r))
                    for r in range(3):
                        raise_max(l, r, r, item(dve, r)[1])
                        less_max(l, r, r)
                    place(l, 0, *item(dve, 4))
                    dve.wait_ge(stored[0], 16 * at(k, 0, HALF) + 16)
                    dve.wait_ge(stored[1], 16 * at(k, 1, HALF))
                    with dve.Fori(0, n) as i:
                        tiles = {0: item(dve, 4 * i)[1]}
                        for r in range(4):
                            q = 4 * i + r
                            evacuate(l, r, q, tiles[r])
                            if r < 2:
                                tiles[r + 3] = item(dve, q + 3)[1]
                            raise_max(l, (r + 3) % 4, q + 3, tiles[r + 3])
                            j, tiles[r + 5] = item(dve, q + 5)
                            place(l, (r + 1) % 4, j, tiles[r + 5])
                            if r < 2:
                                tiles[r + 1] = item(dve, q + 1)[1]
                            less_max(l, (r + 3) % 4, q + 3)
                dve.wait_ge(evac[l], BANKS[l] + RING[l] * n)
                dve.sem_inc(agg_done[l], 1)

            def extend(k, c):
                dve.wait_ge(w_in[k], 16 * KC)
                dve.wait_ge(att_in[k], 32)
                for m in range(2):
                    done(vec.tensor_tensor_reduce(out=Sf[:, 0:D], in0=waiting[c][:, 0:D], in1=attB[:, m, :],
                                                  scale=1.0, scalar=0.0, op0=ALU.mult, op1=ALU.add,
                                                  accum_out=waiting[c][:, D + m:D + m + 1]))

            def linear(l):
                for c in range(KC):
                    dve.wait_ge(split_hi, KC * l + c + 1)
                    w = raw_weights(l, c)
                    width = D if l < 2 else EXT
                    vec.tensor_tensor(wr[:, 1, c, 0:width], w, wr[:, 0, c, 0:width], ALU.subtract).then_inc(split_lo, 1)
                if l != 2:
                    dve.wait_ge(pool_done[l if l < 2 else 2], 1)
                bias = {0: 0, 1: 1, 3: 2}.get(l)
                if bias is not None:
                    dve.wait_ge(bias_in[bias], 16)
                if l == 3:
                    done(vec.reciprocal(rden[:], acc[:, :, ONE]))

                def pre(b, u, t):
                    if l == 3:
                        dve.wait_ge(z_ready[b], OPEN + at(3, b, u))
                        vec.scalar_tensor_tensor(out=ybuf[b], in0=tile(acc, t, D), scalar=rden[:, ds(t, 1)], in1=bB[:],
                                                 op0=ALU.mult, op1=ALU.add).then_inc(z_pre[b], 1)

                def low(b, u, t):
                    dve.wait_ge(zT_ready[b], at(l, b, u) + 1)
                    vec.tensor_tensor(zr[:, b, 1, :], banks(4 + 2 * b, D), zr[:, b, 0, :], ALU.subtract).then_inc(zT_low[b], 1)

                def post(b, u, t):
                    dve.wait_ge(multiplied[b], OPEN + at(l, b, u) + 1)
                    psum = banks(2 * b, EXT)
                    if l < 2:
                        if l == 0:
                            dve.wait_ge(post_act[b], OPEN + at_act(0, b, u))
                        ins = vec.scalar_tensor_tensor(out=ybuf[b], in0=psum[:, 0:D], scalar=dinv[:, ds(t, 1)], in1=bB[:],
                                                       op0=ALU.mult, op1=ALU.add)
                        if l == 0:
                            ins.then_inc(post_dve[b], 1)
                            return
                        ins.then_inc(post_step[b], 1)
                        dve.wait_ge(post_step[b], 2 * at_step(1, b, u) + 1)
                        dve.wait_ge(xr_in[b], 16 * u + 16)
                        vec.tensor_tensor(tile(acc, t, D), ybuf[b], xin[b], ALU.add).then_inc(post_step[b], 1)
                        dve.wait_ge(post_step[b], 2 * at_step(1, b, u) + 2)
                        stats(t).then_inc(post_dve[b], 1)
                        return
                    a = c2[:, b, :]
                    vec.tensor_copy(a, psum[:, D:D + 2]).then_inc(post_step[b], 1)
                    dve.wait_ge(post_step[b], 2 * at_step(l, b, u) + 1)
                    vec.tensor_scalar(acc[:, ds(t, 1), ASRC], a[:, 0:1], 1.0, None, ALU.mult)
                    vec.tensor_scalar(adT[:, ds(t, 1)], a[:, 1:2], 1.0, None, ALU.mult)
                    vec.tensor_tensor(top[:, ds(t, 1)], a[:, 0:1], a[:, 1:2], ALU.add).then_inc(post_step[b], 1)
                    dve.wait_ge(post_step[b], 2 * at_step(l, b, u) + 2)
                    vec.scalar_tensor_tensor(out=mT[:, ds(t, 1)], in0=top[:, ds(t, 1)], scalar=SLOPE, in1=top[:, ds(t, 1)],
                                             op0=ALU.mult, op1=ALU.max).then_inc(post_dve[b], 1)

                if l >= 2:
                    done(vec.memset(acc[:, :, ONE], 1.0))
                pre(0, 0, 0)
                pre(1, 0, 1)
                low(0, 0, 0)

                def steps_of(first, end):
                    with dve.Fori(first, end) as i:
                        for b in range(2):
                            low(1 - b, i + b, 2 * i + b + 1)
                            pre(b, i + 1, 2 * i + b + 2)
                            post(b, i, 2 * i + b)
                if l in (1, 2):
                    steps_of(0, 2)
                    for c in range(KC):
                        extend(l - 1, c)
                        steps_of(2 + c, 3 + c)
                    steps_of(2 + KC, HALF - 1)
                else:
                    steps_of(0, HALF - 1)
                if l == 1:
                    dve.sem_inc(ext_ready[0], 1)
                low(1, HALF - 1, NT - 2)
                pre(0, HALF, NT - 1)
                post(0, HALF - 1, NT - 3)
                low(0, HALF, NT - 1)
                post(1, HALF - 1, NT - 2)
                post(0, HALF, NT - 1)
                if l == 1:
                    dve.wait_ge(post_dve[0], OPEN + at(1, 0, HALF) + 1)
                    aggregate()
                    dve.wait_ge(rooted, 3)
                    done(vec.reciprocal(rstd[:], rstd[:]))
                    done(vec.tensor_copy(lnscale[:], rstd[:]))
                    vec.scalar_tensor_tensor(out=lnbias[:], in0=mv[:, :, 0], scalar=-1.0, in1=rstd[:],
                                             op0=ALU.mult, op1=ALU.mult).then_inc(ln_ready, 1)
                if l == 2:
                    dve.wait_ge(post_dve[0], OPEN + at(2, 0, HALF) + 1)
                    for c in range(KC):
                        ins = vec.tensor_copy(wbuf[:, 1, c, :], waiting[c])
                    done(ins)
                    dve.sem_inc(ext_ready[1], 1)
                if l == 3:
                    dve.wait_ge(post_dve[0], OPEN + at(3, 0, HALF) + 1)

            agg(0)
            linear(0)
            agg(1)
            linear(1)
            linear(2)
            agg(2)
            linear(3)
            agg(3)
            dve.wait_ge(pool_done[3], 1)
            dve.wait_ge(bias_in[3], 16)
            done(vec.reciprocal(rden[:], acc[:, :, ONE]))

            for k, parts in enumerate(x1_parts):
                for t in range(XC * k, XC * k + XC):
                    ins = vec.scalar_tensor_tensor(out=acc[:, t, 0:D], in0=acc[:, t, 0:D], scalar=rden[:, t:t + 1], in1=bB[:],
                                                   op0=ALU.mult, op1=ALU.add)
                ins.then_inc(scaled_out, 1)
                dve.wait_ge(scaled_out, k + 1)
                dve.wait_ge(x1_in[k], 16 * len(parts))
                for buf, first, m in parts:
                    ins = vec.tensor_tensor(acc[:, first:first + m, 0:D], acc[:, first:first + m, 0:D],
                                            buf.rearrange("p (t d) -> p t d", d=D), ALU.add)
                ins.then_inc(summed, 1)

        @block.tensor
        def _(pe):
            mm = nc.tensor.matmul
            open_up(pe, "pe")
            pe.wait_ge(prep, 4)
            pe.wait_ge(edges_f, 2)
            for k in range(2):
                for c in range(EB):
                    ins = nc.tensor.transpose(banks(k)[:, P * c:P * c + P], eflt[k][:, P * c:P * c + P], ident[:])
                ins.then_inc(blocks_turned, 1)
            pe.wait_ge(spans_diag, 1)
            for k in range(2):
                for c in range(EB):
                    o = P * (EB * k + c)
                    ins = mm(banks(2 + k)[:, P * c:P * c + P], ones[:], Sf[:, o:o + P], start=True, stop=True)
                ins.then_inc(spans_wide, 1)
            pe.wait_ge(counts_ready, 1)
            mm(banks(4)[:, 0:1], earlier, wl[:, 13:14], start=True, stop=True)
            mm(banks(4)[:, 1:2], ones[:], wl[:, 13:14], start=True, stop=True).then_inc(offsets_ready, 1)
            for c in range(WORK // 512):
                pe.wait_ge(cover_ready, c + 1)
                if c >= 2:
                    pe.wait_ge(items_kept, c - 1)
                o = PS[0:1, 512 * (5 + 2 * (c % 2)):][:, 0:512]
                held, numbered = covers[c % 2]
                mm(o, wl[:, 17:18], held, start=True, stop=False)
                mm(o, wl[:, 18:19], numbered, start=False, stop=True).then_inc(items_ready, 1)

            def turn_w(k):
                pe.wait_ge(wnat_in, 16 * KC * (1 + k // KC))
                if k >= 2:
                    pe.wait_ge(wt_kept, k - 1)
                for c in range(KC):
                    ins = nc.tensor.transpose(banks(2 * (k % 2), D)[:, P * c:P * c + P], wnat[k % KC][:, P * c:P * c + P], ident[:])
                ins.then_inc(wnat_turned, 1)
            pe.wait_ge(items_kept, WORK // 512)
            for k in range(KC):
                turn_w(k)

            mm(banks(6, NT), zero_b[:], colid_b[:, 0:NT], start=True, stop=False)

            def count(first, end):
                with pe.Fori(first, end) as i:
                    for b in range(2):
                        pe.wait_ge(hots[b], i + 1)
                        for k in range(DB):
                            ins = mm(banks(6, NT), hot_lo[b][:, k, :], hot_hi[b][:, k, 0:NT], start=False, stop=False)
                        ins.then_inc(hots_used[b], 1)
            count(0, BATCHES // 4)
            for k in range(KC, 2 * KC):
                turn_w(k)
            count(BATCHES // 4, BATCHES // 2)
            mm(banks(6, NT), zero_b[:], colid_b[:, 0:NT], start=False, stop=True).then_inc(degrees, 1)
            pe.wait_ge(wt_kept, 2 * KC)

            def product(l, r, s):
                width = D if l < 2 else EXT
                b = 2 * (r % BANKS[l])
                mm(banks(b), sel[r][:, s, :], rows[r][:, s, 0:512], start=(s == 0), stop=(s == G - 1))
                mm(banks(b + 1, width - 512), sel[r][:, s, :], rows[r][:, s, 512:width],
                   start=(s == 0), stop=(s == G - 1)).then_inc(steps[l], 1)

            def turn_v(l, r, q):
                pe.wait_ge(v_ready[l], q + 1)
                for s in range(G):
                    ins = nc.tensor.transpose(banks(4 + r % 2)[:, P * s:P * s + P], V[:, s, :], ident[:])
                ins.then_inc(u_ready[l], 1)

            def widen_m(l, r, q):
                pe.wait_ge(chain[l], CH * q + 5)
                mm(banks(6 + r % 2, P), ones[:], diag[:, r % 2, :], start=True, stop=True).then_inc(m_wide[l], 1)

            def agg(l):
                if l >= 2:
                    def widen_ad(b, u, t, m):
                        pe.wait_ge(ad_diag[b], at_ad(l, b, u) + 1)
                        pe.wait_ge(ad_kept[b], OPEN + at_ad(l, b, u))
                        mm(banks(6 + b, m * P), ones[:], S[:, b, 0:m, :].rearrange(flat), start=True, stop=True).then_inc(ad_wide[b], 1)
                    fours(pe, widen_ad)
                    for q in range(2):
                        turn_v(l, q, q)
                        widen_m(l, q, q)
                n = rounds(pe, l)
                with pe.Fori(0, n) as i:
                    for r in range(RING[l]):
                        q = RING[l] * i + r
                        if l < 2:
                            pe.wait_ge(masked[l], q + 1)
                        else:
                            pe.wait_ge(p_ready[l], 2 + q + 1)
                        pe.wait_ge(evac[l], q + 1)
                        pe.wait_ge(gathered[l][r], 16 * G * i + 16 * G)
                        product(l, r, 0)
                        if l >= 2:
                            turn_v(l, r, q + 2)
                        product(l, r, 1)
                        product(l, r, 2)
                        product(l, r, 3)
                        if l >= 2:
                            widen_m(l, r, q + 2)
                if l >= 2:
                    turn_v(l, 0, 4 * n + 2)
                    widen_m(l, 0, 4 * n + 2)

            def linear(l):
                width = D if l < 2 else EXT

                def turn_z(b, u):
                    pe.wait_ge(z_ready[b], OPEN + at(l, b, u) + 1)
                    pe.wait_ge(zT_low[b], OPEN + at(l, b, u))
                    for c in range(KC):
                        ins = nc.tensor.transpose(banks(4 + 2 * b, D)[:, P * c:P * c + P], zst[b][:, P * c:P * c + P], ident[:])
                    ins.then_inc(turned[b], 1)

                def multiply(b, u):
                    pe.wait_ge(zT_low[b], OPEN + at(l, b, u) + 1)
                    pe.wait_ge(post_dve[b], OPEN + at(l, b, u))
                    if l >= 2:
                        pe.wait_ge(post_act[b], OPEN + at_act(l, b, u))
                    for c in range(KC):
                        for k, (zp, wp) in enumerate(((1, 0), (0, 1), (0, 0))):
                            z = zr[:, b, zp, P * c:P * c + P]
                            first, last = c == 0 and k == 0, c == KC - 1 and k == 2
                            mm(banks(2 * b), z, wr[:, wp, c, 0:512], start=first, stop=last)
                            ins = mm(banks(2 * b + 1, width - 512), z, wr[:, wp, c, 512:width], start=first, stop=last)
                    ins.then_inc(multiplied[b], 1)

                turn_z(0, 0)
                pe.wait_ge(split_lo, KC * l + KC)
                with pe.Fori(0, HALF) as i:
                    for b in range(2):
                        turn_z(1 - b, i + b)
                        multiply(b, i)
                multiply(0, HALF)

            agg(0)
            linear(0)
            agg(1)
            linear(1)
            linear(2)
            agg(2)
            linear(3)
            agg(3)


def kernel(x, src, dst, L0_gnn_W1, L0_gnn_b1, L0_gnn_W2, L0_gnn_b2, L1_gnn_W1, L1_gnn_att_src1, L1_gnn_att_dst1,
           L1_gnn_b1, L1_gnn_W2, L1_gnn_att_src2, L1_gnn_att_dst2, L1_gnn_b2):
    import numpy as np
    import concourse.bacc as bacc
    from concourse.bass_utils import run_bass_kernel_spmd

    given = {
        "x": x, "src": src, "dst": dst,
        "W1": L0_gnn_W1, "b1": L0_gnn_b1, "W2": L0_gnn_W2, "b2": L0_gnn_b2,
        "Wg1": L1_gnn_W1, "as1": L1_gnn_att_src1, "ad1": L1_gnn_att_dst1, "bg1": L1_gnn_b1,
        "Wg2": L1_gnn_W2, "as2": L1_gnn_att_src2, "ad2": L1_gnn_att_dst2, "bg2": L1_gnn_b2,
    }
    nc = bacc.Bacc("TRN2", target_bir_lowering=False, num_devices=1)
    arrays = {f"in_{k}": np.ascontiguousarray(v) for k, v in given.items()}
    args = [nc.dram_tensor(k, a.shape, mybir.dt.from_np(a.dtype), kind="ExternalInput").ap() for k, a in arrays.items()]
    out = nc.dram_tensor("out", arrays["in_x"].shape, F32, kind="ExternalOutput").ap()
    build(nc, *args, out)
    r = run_bass_kernel_spmd(nc, [arrays], core_ids=[0])
    return r.results[0]["out"]
```
